# Optimizing a Trainium2 kernel written in Bass

```python
import numpy as np
import jax
import jax.numpy as jnp

def _softmax(x, axis=-1):
    return jax.nn.softmax(x, axis=axis)
def _gelu(x):
    return jax.nn.gelu(x, approximate=True)
def _silu(x):
    return jax.nn.silu(x)
def _sigmoid(x):
    return jax.nn.sigmoid(x)
def _layernorm(x, axis=-1, eps=1e-5):
    m = jnp.mean(x, axis=axis, keepdims=True)
    v = jnp.var(x, axis=axis, keepdims=True)
    return (x - m) / jnp.sqrt(v + eps)
def _scatter_add(tgt, idx, src, axis=0):
    return tgt.at[idx].add(src)
def _segment_sum(src, seg, n):
    return jax.ops.segment_sum(src, seg, n)

kernel_name = 'mk_metaformer_d1_conv_nchw128_3f357b'

def setup_inputs(seed: int = 0):
    np.random.seed(seed)
    _w = jnp.asarray
    def _rec_inputs():
        import jax
        import jax.numpy as jnp
        _gk = jax.random.key(seed)
        x = -0.0002023 + 1 * jax.random.normal(jax.random.fold_in(_gk, 1), (64, 128, 28, 28), jnp.float32)
        return x
    x = _rec_inputs()
    def _L0_conv_setup():
        import jax, jax.numpy as jnp
        import numpy as np
        B, C, H, W = (64, 128, 28, 28)
        S = H * W
        IC = C // 4
        IS = S // 4
        DS = (1 + IS) // 4
        DC = (1 + IC) // 4

        def _bn(y, s, b):
            return y * s[None, :, None, None] + b[None, :, None, None]

        def _cbr(y, Wc, s, b):
            return jax.nn.relu(_bn(jnp.einsum('oc,bchw->bohw', Wc, y), s, b))
        key = jax.random.key(seed)
        ks = iter(jax.random.split(key, 40))

        def wgt(shape):
            return jax.random.normal(next(ks), shape, jnp.float32) * 0.05

        def scale(c):
            return 1.0 + 0.1 * jax.random.normal(next(ks), (c,), jnp.float32)

        def shift(c):
            return 0.1 * jax.random.normal(next(ks), (c,), jnp.float32)
        inp = {'x': jax.random.normal(next(ks), (B, C, H, W), jnp.float32)}
        for name, shape in [('th_w', (IC, C)), ('ph_w', (IC, C)), ('ggs_w', (IS, 2 * S)), ('gxs_w', (IC, C)), ('ws1_w', (DS, 1 + IS)), ('ws2_w', (1, DS)), ('thc_w', (IS, S)), ('phc_w', (IS, S)), ('ggc_w', (IC, 2 * C)), ('gxc_w', (IS, S)), ('wc1_w', (DC, 1 + IC)), ('wc2_w', (1, DC))]:
            inp[name] = wgt(shape)
        for name, ch in [('th', IC), ('ph', IC), ('ggs', IS), ('gxs', IC), ('ws1', DS), ('ws2', 1), ('thc', IS), ('phc', IS), ('ggc', IC), ('gxc', IS), ('wc1', DC), ('wc2', 1)]:
            inp[name + '_s'] = scale(ch)
            inp[name + '_b'] = shift(ch)
        return inp
    _L0_conv_all = _L0_conv_setup()
    _L0_conv_in = {k: v for k, v in _L0_conv_all.items() if k in ('th_w', 'th_s', 'th_b', 'ph_w', 'ph_s', 'ph_b', 'ggs_w', 'ggs_s', 'ggs_b', 'gxs_w', 'gxs_s', 'gxs_b', 'ws1_w', 'ws1_s', 'ws1_b', 'ws2_w', 'ws2_s', 'ws2_b', 'thc_w', 'thc_s', 'thc_b', 'phc_w', 'phc_s', 'phc_b', 'ggc_w', 'ggc_s', 'ggc_b', 'gxc_w', 'gxc_s', 'gxc_b', 'wc1_w', 'wc1_s', 'wc1_b', 'wc2_w', 'wc2_s', 'wc2_b', )}
    del _L0_conv_all

    def _L0_ffn_setup():
        import jax, jax.numpy as jnp
        import numpy as np
        B, N, D, C, E, K = (8, 8192, 128, 128, 8, 2)
        key = jax.random.key(seed)
        k0, k1, k2 = jax.random.split(key, 3)
        x = jax.random.normal(k0, (B, N, D), dtype=jnp.float32)
        router_w = jax.random.normal(k1, (D, E), dtype=jnp.float32) * 0.05
        router_b = jnp.zeros((E,), dtype=jnp.float32)
        expert_w = jax.random.normal(k2, (E, D, C), dtype=jnp.float32) * (1.0 / np.sqrt(D))
        expert_b = jnp.zeros((E, C), dtype=jnp.float32)
        return {'x': x, 'router_w': router_w, 'router_b': router_b, 'expert_w': expert_w, 'expert_b': expert_b}
    _L0_ffn_all = _L0_ffn_setup()
    _L0_ffn_in = {k: v for k, v in _L0_ffn_all.items() if k in ('router_w', 'router_b', 'expert_w', 'expert_b', )}
    del _L0_ffn_all

    return {
        "x": x,
        "L0_conv_th_w": _L0_conv_in["th_w"],
        "L0_conv_th_s": _L0_conv_in["th_s"],
        "L0_conv_th_b": _L0_conv_in["th_b"],
        "L0_conv_ph_w": _L0_conv_in["ph_w"],
        "L0_conv_ph_s": _L0_conv_in["ph_s"],
        "L0_conv_ph_b": _L0_conv_in["ph_b"],
        "L0_conv_ggs_w": _L0_conv_in["ggs_w"],
        "L0_conv_ggs_s": _L0_conv_in["ggs_s"],
        "L0_conv_ggs_b": _L0_conv_in["ggs_b"],
        "L0_conv_gxs_w": _L0_conv_in["gxs_w"],
        "L0_conv_gxs_s": _L0_conv_in["gxs_s"],
        "L0_conv_gxs_b": _L0_conv_in["gxs_b"],
        "L0_conv_ws1_w": _L0_conv_in["ws1_w"],
        "L0_conv_ws1_s": _L0_conv_in["ws1_s"],
        "L0_conv_ws1_b": _L0_conv_in["ws1_b"],
        "L0_conv_ws2_w": _L0_conv_in["ws2_w"],
        "L0_conv_ws2_s": _L0_conv_in["ws2_s"],
        "L0_conv_ws2_b": _L0_conv_in["ws2_b"],
        "L0_conv_thc_w": _L0_conv_in["thc_w"],
        "L0_conv_thc_s": _L0_conv_in["thc_s"],
        "L0_conv_thc_b": _L0_conv_in["thc_b"],
        "L0_conv_phc_w": _L0_conv_in["phc_w"],
        "L0_conv_phc_s": _L0_conv_in["phc_s"],
        "L0_conv_phc_b": _L0_conv_in["phc_b"],
        "L0_conv_ggc_w": _L0_conv_in["ggc_w"],
        "L0_conv_ggc_s": _L0_conv_in["ggc_s"],
        "L0_conv_ggc_b": _L0_conv_in["ggc_b"],
        "L0_conv_gxc_w": _L0_conv_in["gxc_w"],
        "L0_conv_gxc_s": _L0_conv_in["gxc_s"],
        "L0_conv_gxc_b": _L0_conv_in["gxc_b"],
        "L0_conv_wc1_w": _L0_conv_in["wc1_w"],
        "L0_conv_wc1_s": _L0_conv_in["wc1_s"],
        "L0_conv_wc1_b": _L0_conv_in["wc1_b"],
        "L0_conv_wc2_w": _L0_conv_in["wc2_w"],
        "L0_conv_wc2_s": _L0_conv_in["wc2_s"],
        "L0_conv_wc2_b": _L0_conv_in["wc2_b"],
        "L0_ffn_router_w": _L0_ffn_in["router_w"],
        "L0_ffn_router_b": _L0_ffn_in["router_b"],
        "L0_ffn_expert_w": _L0_ffn_in["expert_w"],
        "L0_ffn_expert_b": _L0_ffn_in["expert_b"],
    }

def reference(x, L0_conv_th_w, L0_conv_th_s, L0_conv_th_b, L0_conv_ph_w, L0_conv_ph_s, L0_conv_ph_b, L0_conv_ggs_w, L0_conv_ggs_s, L0_conv_ggs_b, L0_conv_gxs_w, L0_conv_gxs_s, L0_conv_gxs_b, L0_conv_ws1_w, L0_conv_ws1_s, L0_conv_ws1_b, L0_conv_ws2_w, L0_conv_ws2_s, L0_conv_ws2_b, L0_conv_thc_w, L0_conv_thc_s, L0_conv_thc_b, L0_conv_phc_w, L0_conv_phc_s, L0_conv_phc_b, L0_conv_ggc_w, L0_conv_ggc_s, L0_conv_ggc_b, L0_conv_gxc_w, L0_conv_gxc_s, L0_conv_gxc_b, L0_conv_wc1_w, L0_conv_wc1_s, L0_conv_wc1_b, L0_conv_wc2_w, L0_conv_wc2_s, L0_conv_wc2_b, L0_ffn_router_w, L0_ffn_router_b, L0_ffn_expert_w, L0_ffn_expert_b):
    import jax
    import jax.numpy as jnp
    def _L0_conv_ref(x, th_w, th_s, th_b, ph_w, ph_s, ph_b, ggs_w, ggs_s, ggs_b, gxs_w, gxs_s, gxs_b, ws1_w, ws1_s, ws1_b, ws2_w, ws2_s, ws2_b, thc_w, thc_s, thc_b, phc_w, phc_s, phc_b, ggc_w, ggc_s, ggc_b, gxc_w, gxc_s, gxc_b, wc1_w, wc1_s, wc1_b, wc2_w, wc2_s, wc2_b):
        import jax, jax.numpy as jnp
        import numpy as np
        B, C, H, W = (64, 128, 28, 28)
        S = H * W
        IC = C // 4
        IS = S // 4
        DS = (1 + IS) // 4
        DC = (1 + IC) // 4

        def _bn(y, s, b):
            return y * s[None, :, None, None] + b[None, :, None, None]

        def _cbr(y, Wc, s, b):
            return jax.nn.relu(_bn(jnp.einsum('oc,bchw->bohw', Wc, y), s, b))
        b, c, h, w = x.shape
        hw = h * w
        theta = _cbr(x, th_w, th_s, th_b).reshape(b, -1, hw)
        phi = _cbr(x, ph_w, ph_s, ph_b).reshape(b, -1, hw)
        Gs = jnp.einsum('bci,bcj->bij', theta, phi)
        Gs_in = jnp.transpose(Gs, (0, 2, 1)).reshape(b, hw, h, w)
        Gs_out = Gs.reshape(b, hw, h, w)
        Gs_joint = _cbr(jnp.concatenate([Gs_in, Gs_out], 1), ggs_w, ggs_s, ggs_b)
        g_xs = jnp.mean(_cbr(x, gxs_w, gxs_s, gxs_b), axis=1, keepdims=True)
        ys = jnp.concatenate([g_xs, Gs_joint], 1)
        W_ys = _bn(jnp.einsum('oc,bchw->bohw', ws2_w, _cbr(ys, ws1_w, ws1_s, ws1_b)), ws2_s, ws2_b)
        x = jax.nn.sigmoid(W_ys) * x
        xc = jnp.transpose(x.reshape(b, c, hw), (0, 2, 1))[..., None]
        theta_c = jnp.transpose(_cbr(xc, thc_w, thc_s, thc_b)[..., 0], (0, 2, 1))
        phi_c = _cbr(xc, phc_w, phc_s, phc_b)[..., 0]
        Gc = jnp.einsum('bcs,bsd->bcd', theta_c, phi_c)
        Gc_joint = _cbr(jnp.concatenate([jnp.transpose(Gc, (0, 2, 1))[..., None], Gc[..., None]], 1), ggc_w, ggc_s, ggc_b)
        g_xc = jnp.mean(_cbr(xc, gxc_w, gxc_s, gxc_b), axis=1, keepdims=True)
        yc = jnp.concatenate([g_xc, Gc_joint], 1)
        W_yc = _bn(jnp.einsum('oc,bchw->bohw', wc2_w, _cbr(yc, wc1_w, wc1_s, wc1_b)), wc2_s, wc2_b)
        W_yc = jnp.transpose(W_yc, (0, 2, 1, 3))
        return jax.nn.sigmoid(W_yc) * x

    def _L0_ffn_ref(x, router_w, router_b, expert_w, expert_b):
        import jax, jax.numpy as jnp
        import numpy as np
        B, N, D, C, E, K = (8, 8192, 128, 128, 8, 2)
        router_probs = jax.nn.softmax(x @ router_w + router_b, axis=-1)
        top_p, top_i = jax.lax.top_k(router_probs, K)
        top_p = top_p / jnp.sum(top_p, axis=-1, keepdims=True)
        expert_out = jnp.einsum('bnd,edc->bnec', x, expert_w) + expert_b
        gathered = jnp.take_along_axis(expert_out, top_i[..., None], axis=2)
        return jnp.einsum('bnk,bnkc->bnc', top_p, gathered)

    def _gn(v, G=32, eps=1e-5):
        B_, C_, H_, W_ = v.shape
        g = v.reshape(B_, G, C_ // G, H_, W_)
        m = jnp.mean(g, axis=(2, 3, 4), keepdims=True)
        s = jnp.var(g, axis=(2, 3, 4), keepdims=True)
        return ((g - m) / jnp.sqrt(s + eps)).reshape(v.shape)

    def _ln_c(v, eps=1e-6):
        m = jnp.mean(v, axis=1, keepdims=True)
        s = jnp.var(v, axis=1, keepdims=True)
        return (v - m) / jnp.sqrt(s + eps)

    def _ln_t(v, eps=1e-5):
        m = jnp.mean(v, axis=-1, keepdims=True)
        s = jnp.var(v, axis=-1, keepdims=True)
        return (v - m) / jnp.sqrt(s + eps)

    def _to_tokens(v):
        B_, C_, H_, W_ = v.shape
        return v.reshape(B_, C_, H_ * W_).transpose(0, 2, 1)
    def _from_tokens(t, like):
        B_, C_, H_, W_ = like.shape
        return t.transpose(0, 2, 1).reshape(B_, C_, H_, W_)

    x = x + _L0_conv_ref(_ln_c(x), L0_conv_th_w, L0_conv_th_s, L0_conv_th_b, L0_conv_ph_w, L0_conv_ph_s, L0_conv_ph_b, L0_conv_ggs_w, L0_conv_ggs_s, L0_conv_ggs_b, L0_conv_gxs_w, L0_conv_gxs_s, L0_conv_gxs_b, L0_conv_ws1_w, L0_conv_ws1_s, L0_conv_ws1_b, L0_conv_ws2_w, L0_conv_ws2_s, L0_conv_ws2_b, L0_conv_thc_w, L0_conv_thc_s, L0_conv_thc_b, L0_conv_phc_w, L0_conv_phc_s, L0_conv_phc_b, L0_conv_ggc_w, L0_conv_ggc_s, L0_conv_ggc_b, L0_conv_gxc_w, L0_conv_gxc_s, L0_conv_gxc_b, L0_conv_wc1_w, L0_conv_wc1_s, L0_conv_wc1_b, L0_conv_wc2_w, L0_conv_wc2_s, L0_conv_wc2_b)
    t = _to_tokens(x)
    t = t + _L0_ffn_ref(_ln_t(t), L0_ffn_router_w, L0_ffn_router_b, L0_ffn_expert_w, L0_ffn_expert_b)
    x = _from_tokens(t, x)
    return x


_drawn_inputs = setup_inputs


def setup_inputs(seed=0):
    import zlib

    import numpy as np

    out = dict(_drawn_inputs(seed))
    spreads = {'L0_ffn_router_b': (0.0, 0.1), 'L0_ffn_expert_b': (0.0, 0.1)}
    factors = {'L0_conv_th_w': 28.768,
     'L0_conv_th_s': 64.0,
     'L0_conv_th_b': 8.0,
     'L0_conv_ph_w': 27.072,
     'L0_conv_ph_s': 64.0,
     'L0_conv_ph_b': 64.0,
     'L0_conv_ggs_w': 27.512,
     'L0_conv_ggs_s': 64.0,
     'L0_conv_ggs_b': 8.0,
     'L0_conv_gxs_w': 8.0,
     'L0_conv_gxs_s': 8.0,
     'L0_conv_gxs_b': 8.0,
     'L0_conv_ws1_s': 64.0,
     'L0_conv_ws1_b': 8.0,
     'L0_conv_thc_s': 46.784,
     'L0_conv_thc_b': 48.944,
     'L0_conv_phc_s': 52.368,
     'L0_conv_phc_b': 48.576,
     'L0_conv_ggc_s': 44.096,
     'L0_conv_ggc_b': 64.0,
     'L0_conv_gxc_w': 64.0,
     'L0_conv_gxc_s': 64.0,
     'L0_conv_gxc_b': 8.0,
     'L0_conv_wc1_s': 35.256,
     'L0_conv_wc1_b': 64.0,
     'L0_conv_ws1_w': 8.0,
     'L0_conv_ws2_w': 8.0,
     'L0_conv_thc_w': 8.0,
     'L0_conv_phc_w': 8.0}
    for name, (base, spread) in spreads.items():
        noise = np.random.default_rng([zlib.crc32(name.encode()), seed]).standard_normal(out[name].shape)
        drawn = base * np.exp(spread * noise) if base else spread * noise
        out[name] = jnp.asarray(drawn.astype(out[name].dtype))
    for name, factor in factors.items():
        out[name] = (out[name] * factor).astype(out[name].dtype)
    return out
```

```python
from contextlib import ExitStack

import concourse.bass as bass
from concourse import mybir

ALU = mybir.AluOpType
ACT = mybir.ActivationFunctionType
F32 = mybir.dt.float32
F32R = mybir.dt.float32r
BF16 = mybir.dt.bfloat16
AX_X = mybir.AxisListType.X

BATCH, C, HH, WW = 64, 128, 28, 28
S = HH * WW
T, NT = 112, 7
IC, IS = C // 4, S // 4
DS, DC = (1 + IS) // 4, (1 + IC) // 4
E = 8
PAIR = 2
UNITS = BATCH // PAIR
QUART = ((0, 4), (4, 7))
TAIL = IS - C
GX3, GX4 = C - TAIL, C - TAIL
GX5 = IS - GX3 - GX4
MT = 5
KR = 12 * E
EPS1, EPS2 = 1e-6, 1e-5
BIG = 1e30

USES = (
    [(f"x_tok{b}{q}", "y_tok_ready", 2 * b + q + 1) for b in range(2) for q in range(2)]
    + [(f"y_ch{b}{q}", "y_ch_ready", 2 * b + q + 1) for b in range(2) for q in range(2)]
    + [(f"tp{b}{q}", "tp_ready", 2 * b + q + 1) for b in range(2) for q in range(2)]
    + [(f"tp_tok{q}", "tp_tok_ready", q + 1) for q in range(2)]
    + [("mix", "mix_ready", 1)]
    + [("joint000", "joint_ready", 1), ("joint001", "joint_ready", 2),
       ("joint010", "joint_ready", 3), ("joint011", "joint_ready", 4),
       ("hid00", "hid_ready", 1),
       ("joint100", "joint_ready", 5), ("joint101", "joint_ready", 6),
       ("hid01", "hid_ready", 2),
       ("joint110", "joint_ready", 7), ("joint111", "joint_ready", 8),
       ("hid10", "hid_ready", 3), ("hid11", "hid_ready", 4)]
    + [("slogit", "slogit_read", 1)]
    + [(f"chan{m}", "chan_ready", m + 1) for m in range(3)]
    + [("gram", "gram_ready", 1), ("jc", "jc_ready", 1), ("hc", "hc_ready", 1), ("clogit", "clogit_read", 1)]
    + [(f"x1_ch{b}{q}", "x2_ready", 2 * b + q + 1) for b in range(2) for q in range(2)]
    + [(f"x2_tok{b}{q}", "stats2_ready", 2 * b + q + 1) for b in range(2) for q in range(2)]
    + [(f"mean{b}{q}", "centred_ready", 2 * b + q + 1) for b in range(2) for q in range(2)]
    + [("rlogit", "rlogit_read", 1)]
    + [(f"gates{b}", "gates_ready", b + 1) for b in range(2)]
)
INDEX = {u[0]: n for n, u in enumerate(USES)}
NU = len(USES)
NB = 4
assert (2 * NU) % NB == 0
PER = {"bank_filled": NU}
for _name, _sem, _k in USES:
    PER[_sem] = max(PER.get(_sem, 0), _k)
PER.update(stat=12, stats1_ready=1, rstd1_ready=1, rstd2_ready=1, mean2_ready=1, szlogit_ready=1, sexp_ready=1,
           x1_ready=1, x1_hi_ready=1, x1_lo_ready=1, czlogit_ready=1, cexp_ready=1, cgate=2, sgate=2,
           rgap_ready=1, rexp_ready=1, gatev_ready=1, route=21, part=8,
           gate_seen=32, prod_ready=32, hi_ready=32, lo_ready=32, exp_done=32, out_ready=4)

NEXP = 4 * E
LAG = 2
RING = 3
PIECES = [(b, q) for b in range(2) for q in range(2)]


def cols(q):
    return slice(QUART[q][0] * T, QUART[q][1] * T)


def metaformer_kernel(nc, a, out):
    with ExitStack() as ctx:
        def sb(name, shape, dt=F32):
            return ctx.enter_context(nc.sbuf_tensor(name, shape, dt))

        sems = {}

        def sem(name):
            if name not in sems:
                sems[name] = ctx.enter_context(nc.semaphore(name))
            return sems[name]

        rot = [ctx.enter_context(nc.psum_tensor(f"rot{i}", [128, 512], F32)) for i in range(NB)]
        gbank = [ctx.enter_context(nc.psum_tensor(f"gbank{i}", [128, 512], F32)) for i in range(RING)]
        acc = ctx.enter_context(nc.psum_tensor("acc", [128, 512], F32))

        ident = sb("ident", [128, 128])
        identb = sb("identb", [128, 128], BF16)
        w3 = sb("w3", [C, 3 * IC])
        b3 = sb("b3", [3 * IC, 1])
        wggs = sb("wggs", [T, NT, 2 * IS])
        bggs = sb("bggs", [128, 2])
        wws1 = sb("wws1", [128, 2, DS])
        bws1 = sb("bws1", [DS, 1])
        wws2 = sb("wws2", [DS, 1])
        sbs = sb("sbs", [T, 2])
        wch = sb("wch", [T, NT, MT * 128], F32R)
        wcl = sb("wcl", [T, NT, MT * 128], F32R)
        bc = sb("bc", [128, MT])
        wggc = sb("wggc", [C, 2, IC])
        bggc = sb("bggc", [IC, 1])
        wwc1 = sb("wwc1", [IC, DC])
        wwc1g = sb("wwc1g", [128, 3, DC])
        bwc1 = sb("bwc1", [DC, 1])
        wwc2 = sb("wwc2", [DC, 1])
        sbc = sb("sbc", [C, 2])
        wr = sb("wr", [C, E])
        rb = sb("rb", [T, E])
        pref = sb("pref", [T, E])
        weh = sb("weh", [C, E, C], F32R)
        wel = sb("wel", [C, E, C], F32R)
        selg = sb("selg", [KR, E, 128], BF16)
        bstk = sb("bstk", [KR, C], BF16)
        one = sb("one", [T, 1])
        mhalf = sb("mhalf", [T, 2 * NT])

        x = [sb(f"xin{p}", [C, PAIR, S]) for p in range(2)]
        x2 = [sb(f"x2_{p}", [C, PAIR, S]) for p in range(2)]
        cen = [sb(f"cen{p}", [C, PAIR, S]) for p in range(2)]
        gt = [sb(f"gt{p}", [KR, PAIR, S], BF16) for p in range(2)]
        st = sb("st", [T, 2 * NT, 6])
        sm = sb("sm", [T, 6, 2 * NT])
        mean1 = sb("mean1", [T, 2 * NT])
        var1 = sb("var1", [T, 2 * NT])
        rstd1 = sb("rstd1", [T, 2 * NT])
        mean2 = sb("mean2", [T, 2 * NT])
        var2 = sb("var2", [T, 2 * NT])
        rstd2 = sb("rstd2", [T, 2 * NT])
        y_tok = sb("y_tok", [T, NT, PAIR, C])
        y_ch = sb("y_ch", [C, PAIR, S])
        tp = sb("tp", [128, S])
        tp_tok = sb("tp_tok", [T, NT, 128])
        mix = sb("mix", [128, IS])
        j1 = sb("j1", [128, PAIR, S])
        j2 = sb("j2", [128, PAIR, S])
        hid = sb("hid", [DS, PAIR, S])
        sz = sb("sz", [T, 2 * NT])
        se = sb("se", [T, 2 * NT])
        sp1 = sb("sp1", [T, 2 * NT])
        sig = sb("sig", [T, 2 * NT])
        x1 = sb("x1", [T, NT, PAIR, C])
        x1h = sb("x1h", [T, NT, PAIR, C], F32R)
        x1l = sb("x1l", [T, NT, PAIR, C], F32R)
        chan = sb("chan", [128, MT, PAIR, C])
        gram = sb("gram", [C, 2, PAIR, C])
        jc = sb("jc", [IC, PAIR, C])
        hc = sb("hc", [DC, PAIR, C])
        cz = sb("cz", [C, 4, PAIR])
        cg = sb("cg", [C, PAIR])
        lg = sb("lg", [T, 2 * NT, E])
        lg2 = sb("lg2", [T, 2 * NT, E])
        eq = sb("eq", [T, 2 * NT, E])
        first = sb("first", [T, 2 * NT, E])
        second = sb("second", [T, 2 * NT, E])
        mx = sb("mx", [T, 8, 2 * NT])
        gv = sb("gv", [T, 2 * NT, 2, E])
        gs = sb("gs", [T, 2 * NT, 3, 4, E], BF16)
        prod_h = sb("prod_h", [C, RING, 448], F32R)
        prod_l = sb("prod_l", [C, RING, 448], F32R)

        block = ctx.enter_context(nc.Block())

        def need(eng, name, k, p, n, back=0):
            if isinstance(k, int) and 2 * k + p - back < 0:
                return
            eng.wait_ge(sem(name), k * (2 * PER[name]) + ((p - back) * PER[name] + n))

        def bank(use, p):
            return rot[(p * NU + INDEX[use]) % NB]

        def free(eng, use, k, p):
            n = INDEX[use] - NB
            _, s, c = USES[n % NU]
            need(eng, s, k, p, c, back=int(n < 0))

        def filled(eng, use, k, p):
            need(eng, "bank_filled", k, p, INDEX[use] + 1)

        def units(eng, step, last=UNITS):
            step(eng, 0, 0)
            step(eng, 0, 1)
            with eng.Fori(1, last // 2) as k:
                step(eng, k, 0)
                step(eng, k, 1)

        raw_c = [x2[0], x2[1]]
        rawc_all = [x2[0][:, 0, :], x2[0][:, 1, :], x2[1][:, 0, :], x2[1][:, 1, :], cen[0][:, 0, :]]
        raw_ggs = [cen[1][0:98, :, :].rearrange("p b s -> p (b s)"), y_ch[0:98, :, :].rearrange("p b s -> p (b s)")]
        raw_w3 = tp_raw = sb("raw_w3", [3 * IC, C])
        raw_s3 = sb("raw_s3", [3 * IC, 1])
        raw_sggs = sb("raw_sggs", [98, 2])
        raw_ws1 = sb("raw_ws1", [DS, 1 + IS])
        pad_ws1 = sb("pad_ws1", [DS, 256])
        raw_sws1 = sb("raw_sws1", [DS, 1])
        raw_sbs = sb("raw_sbs", [T, 2])
        raw_sc = sb("raw_sc", [128, MT])
        raw_ggc = sb("raw_ggc", [IC, 2 * C])
        raw_sggc = sb("raw_sggc", [IC, 1])
        raw_wc1 = sb("raw_wc1", [DC, 1 + IC])
        pad_wc1 = sb("pad_wc1", [DC, 3, 128])
        raw_swc1 = sb("raw_swc1", [DC, 1])
        raw_sbc = sb("raw_sbc", [C, 2])
        raw_we = j1[:, :, :].rearrange("p b s -> p (b s)")[:, 0:E * C].rearrange("p (e c) -> p e c", e=E)
        raw_eb = sb("raw_eb", [E, C])
        res_eb = sb("res_eb", [E, C])
        eb = sb("eb", [E, 3, C], BF16)

        def col(v):
            return v.rearrange("(n o) -> n o", o=1)

        def spread(v, n):
            return v.rearrange("(o n) -> o n", o=1).partition_broadcast(n) if False else v.partition_broadcast(n)

        x_dram = a["x"].rearrange("n c h w -> n c (h w)")
        o_dram = out.rearrange("n c h w -> n c (h w)")

        small = [
            (raw_w3[0:32, :], a["th_w"]), (raw_w3[32:64, :], a["ph_w"]), (raw_w3[64:96, :], a["gxs_w"]),
            (raw_s3[0:32, :], col(a["th_s"])), (raw_s3[32:64, :], col(a["ph_s"])), (raw_s3[64:96, :], col(a["gxs_s"])),
            (b3[0:32, :], col(a["th_b"])), (b3[32:64, :], col(a["ph_b"])), (b3[64:96, :], col(a["gxs_b"])),
            (raw_ggs[0], a["ggs_w"][0:98, :]), (raw_ggs[1], a["ggs_w"][98:196, :]),
            (raw_sggs[:, 0:1], col(a["ggs_s"][0:98])), (raw_sggs[:, 1:2], col(a["ggs_s"][98:196])),
            (bggs[0:128, 0:1], col(a["ggs_b"][0:128])), (bggs[0:TAIL, 1:2], col(a["ggs_b"][128:196])),
            (raw_ws1[:, :], a["ws1_w"]), (raw_sws1[:, :], col(a["ws1_s"])), (bws1[:, :], col(a["ws1_b"])),
            (wws2[:, :], a["ws2_w"].rearrange("o n -> n o")),
            (raw_sbs[:, 0:1], a["ws2_s"].partition_broadcast(T)), (raw_sbs[:, 1:2], a["ws2_b"].partition_broadcast(T)),
            (raw_ggc[:, :], a["ggc_w"]), (raw_sggc[:, :], col(a["ggc_s"])), (bggc[:, :], col(a["ggc_b"])),
            (raw_wc1[:, :], a["wc1_w"]), (raw_swc1[:, :], col(a["wc1_s"])), (bwc1[:, :], col(a["wc1_b"])),
            (wwc2[:, :], a["wc2_w"].rearrange("o n -> n o")),
            (raw_sbc[:, 0:1], a["wc2_s"].partition_broadcast(C)), (raw_sbc[:, 1:2], a["wc2_b"].partition_broadcast(C)),
            (wr[:, :], a["router_w"]), (rb[:, :], a["router_b"].partition_broadcast(T)),
            (raw_we, a["expert_w"].rearrange("e d c -> d e c")), (raw_eb[:, :], a["expert_b"]),
        ]
        stack = [(0, 0, "thc", 0, 128), (1, 0, "phc", 0, 128), (2, 0, "thc", 128, IS), (3, 0, "phc", 128, IS),
                 (2, TAIL, "gxc", 0, GX3), (3, TAIL, "gxc", GX3, GX3 + GX4), (4, 0, "gxc", GX3 + GX4, IS)]
        for m, r, w, lo, hi in stack:
            small += [(rawc_all[m][r:r + hi - lo, :], a[w + "_w"][lo:hi, :]),
                      (raw_sc[r:r + hi - lo, m:m + 1], col(a[w + "_s"][lo:hi])),
                      (bc[r:r + hi - lo, m:m + 1], col(a[w + "_b"][lo:hi]))]

        def load_x(eng, k, p):
            u2 = (2 * k + p) * PAIR
            eng.dma_start(x[p][:, :, :], x_dram[bass.ds(u2, PAIR)].rearrange("b c s -> c b s"))\
               .then_inc(sem(f"x_loaded{p}"), 16)

        def store(eng, k, p, b):
            need(eng, "out_ready", k, p, 2 * b + 2, back=1)
            img = (2 * k + p - 1) * PAIR + b
            eng.dma_start(o_dram[bass.ds(img, 1)].rearrange("b c s -> c b s"), x2[1 - p][:, b:b + 1, :])\
               .then_inc(sem(f"stored{1 - p}"), 16)

        @block.sync
        def _(sp):
            load_x(sp, 0, 0)
            sp.wait_ge(sem("zeroed"), 3)
            for dst, src in small:
                sp.dma_start(dst, src).then_inc(sem("weights_loaded"), 16)
            load_x(sp, 0, 1)
            sp.wait_ge(sem("bias_parts_ready"), 3)
            sp.wait_ge(sem("cleared"), 4)
            for i in range(3):
                for j in range(3):
                    r = 4 * E * i + E * (1 + j)
                    sp.dma_start(bstk[r:r + E, :], eb[:, j, :]).then_inc(sem("bias_stacked"), 16)

            def step(sp, k, p, more=True):
                if not isinstance(k, int) or 2 * k + p > 0:
                    store(sp, k, p, 0)
                if more:
                    need(sp, "x2_ready", k, p, 4)
                    load_x(sp, k + 1, p)
                if not isinstance(k, int) or 2 * k + p > 0:
                    store(sp, k, p, 1)

            units(sp, step, last=UNITS - 2)
            step(sp, UNITS // 2 - 1, 0, more=False)
            step(sp, UNITS // 2 - 1, 1, more=False)
            store(sp, UNITS // 2, 0, 0)
            store(sp, UNITS // 2, 0, 1)
            for p in range(2):
                sp.wait_ge(sem(f"stored{p}"), 16 * PAIR * UNITS // 2)

        @block.gpsimd
        def _(pool):
            nc.gpsimd.memset(cen[0][:, 0, :], 0.0).then_inc(sem("zeroed"), 1)
            nc.gpsimd.memset(raw_sc[:, :], 0.0).then_inc(sem("zeroed"), 1)
            nc.gpsimd.memset(bc[:, :], 0.0).then_inc(sem("zeroed"), 1)
            nc.gpsimd.memset(bstk[:, :], 0.0).then_inc(sem("cleared"), 1)
            pool.wait_ge(sem("zeroed"), 3)
            pool.wait_ge(sem("cleared"), 1)
            nc.gpsimd.memset(j2[64:96, :, :], 0.0).then_inc(sem("cleared"), 1)
            pool.wait_ge(sem("cleared"), 2)
            nc.gpsimd.memset(one[:, :], 1.0).then_inc(sem("cleared"), 1)
            nc.gpsimd.memset(mhalf[:, :], -0.5).then_inc(sem("cleared"), 1)
            nc.gpsimd.memset(ident[:, :], 0.0).then_inc(sem("ident_ready"), 1)
            nc.gpsimd.memset(selg[:, :, :], 0.0).then_inc(sem("sel_ready"), 1)
            pool.wait_ge(sem("ident_ready"), 1)
            nc.gpsimd.affine_select(out=ident[:, :], in_=ident[:, :], compare_op=ALU.not_equal, fill=1.0,
                                    base=0, pattern=[[-1, 128]], channel_multiplier=1).then_inc(sem("ident_ready"), 1)
            pool.wait_ge(sem("ident_ready"), 2)
            nc.gpsimd.tensor_copy(identb[:, :], ident[:, :]).then_inc(sem("ident_ready"), 1)
            for i in range(3):
                pool.wait_ge(sem("sel_ready"), i + 1)
                nc.gpsimd.affine_select(out=selg[:, :, :], in_=selg[:, :, :], compare_op=ALU.not_equal, fill=1.0,
                                        base=-4 * E * i, pattern=[[-1, E], [0, 128]], channel_multiplier=1)\
                    .then_inc(sem("sel_ready"), 1)

            def step(pool, k, p):
                need(pool, "stats1_ready", k, p, 1)
                if isinstance(k, int) and k + p == 0:
                    pool.wait_ge(sem("cleared"), 4)
                nc.gpsimd.tensor_tensor(rstd1[:, :], var1[:, :], mhalf[:, :], ALU.pow).then_inc(sem("rstd1_ready"), 1)
                need(pool, "x1_hi_ready", k, p, 1)
                nc.gpsimd.tensor_tensor(x1l[:, :, :, :], x1[:, :, :, :], x1h[:, :, :, :].bitcast(F32), ALU.subtract)\
                    .then_inc(sem("x1_lo_ready"), 1)
                need(pool, "mean2_ready", k, p, 1)
                nc.gpsimd.tensor_tensor(rstd2[:, :], var2[:, :], mhalf[:, :], ALU.pow).then_inc(sem("rstd2_ready"), 1)
                need(pool, "gatev_ready", k, p, 1)
                n = 0
                ones2 = one[:, :].unsqueeze(1).unsqueeze(1).to_broadcast([T, 2 * NT, 2, E])
                for i in range(3):
                    nc.gpsimd.tensor_tensor(gs[:, :, i, 0:2, :], gv[:, :, :, :], ones2, ALU.mult).then_inc(sem("part"), 1)
                    n += 1
                    need(pool, "part", k, p, n)
                    nc.gpsimd.tensor_tensor(gs[:, :, i, 2:4, :], gs[:, :, i, 1:2, :].to_broadcast([T, 2 * NT, 2, E]),
                                            ones2, ALU.mult).then_inc(sem("part"), 1)
                    n += 1
                    if i < 2:
                        nc.gpsimd.tensor_tensor(gv[:, :, :, :], gv[:, :, :, :], gs[:, :, i, 0:2, :], ALU.subtract)\
                            .then_inc(sem("part"), 1)
                        n += 1
                        need(pool, "part", k, p, n)
                assert n == PER["part"]

            units(pool, step)

        @block.scalar
        def _(act):
            n = 0
            for j in range(NT):
                for m in range(2):
                    act.wait_ge(sem("prep_filled"), n + 1)
                    half = rot[n % NB]
                    nc.scalar.copy(wggs[:, j, 98 * m:98 * m + 98], half[0:T, 0:98])
                    nc.scalar.copy(wggs[:, j, IS + 98 * m:IS + 98 * m + 98], half[0:T, 98:196])\
                        .then_inc(sem("prep_read"), 1)
                    n += 1
            for m in range(MT):
                for j0, j1_ in QUART:
                    act.wait_ge(sem("prep_filled"), n + 1)
                    src = rot[n % NB][0:T, 0:(j1_ - j0) * 128].rearrange("p (j c) -> p j c", c=128)
                    nc.scalar.copy(wch[:, j0:j1_, m * 128:(m + 1) * 128], src).then_inc(sem("wch_ready"), 1)
                    n += 1
            act.wait_ge(sem("weights_loaded"), 16 * len(small))
            nc.scalar.copy(weh[:, :, :], raw_we).then_inc(sem("weh_ready"), 1)

            def experts(act, k, p, lo, hi):
                for n in range(lo, min(hi, NEXP)):
                    q = (n // E) % 2
                    w = (QUART[q][1] - QUART[q][0]) * T
                    need(act, "prod_ready", k, p, n + 1, back=1)
                    if n >= RING:
                        need(act, "exp_done", k, p, n + 1 - RING, back=1)
                    nc.scalar.copy(prod_h[:, n % RING, 0:w], gbank[n % RING][:, 0:w]).then_inc(sem("hi_ready"), 1)

            def step(act, k, p):
                ex = not isinstance(k, int) or 2 * k + p > 0

                def items(lo, hi):
                    if ex:
                        experts(act, k, p, lo, hi)

                items(0, 3)
                for b, q in PIECES:
                    filled(act, f"y_ch{b}{q}", k, p)
                    w = (QUART[q][1] - QUART[q][0]) * T
                    nc.scalar.copy(y_ch[:, b, cols(q)], bank(f"y_ch{b}{q}", p)[:, 0:w]).then_inc(sem("y_ch_ready"), 1)
                items(3, 5)
                for b, q in PIECES:
                    filled(act, f"tp{b}{q}", k, p)
                    src = bank(f"tp{b}{q}", p)
                    w = (QUART[q][1] - QUART[q][0]) * T
                    nc.scalar.activation(tp[64 * b:64 * b + 64, cols(q)], src[0:2 * IC, 0:w], ACT.Relu, bias=b3[0:2 * IC, :])
                    nc.scalar.activation(j2[96:128, b, cols(q)], src[2 * IC:3 * IC, 0:w], ACT.Relu,
                                         bias=b3[2 * IC:3 * IC, :]).then_inc(sem("tp_ready"), 1)
                items(5, 7)
                for q in range(2):
                    filled(act, f"tp_tok{q}", k, p)
                    j0, jn = QUART[q]
                    src = bank(f"tp_tok{q}", p)[0:T, 0:(jn - j0) * 128].rearrange("p (j c) -> p j c", c=128)
                    nc.scalar.copy(tp_tok[:, j0:jn, :], src).then_inc(sem("tp_tok_ready"), 1)
                items(7, 9)
                filled(act, "mix", k, p)
                src = bank("mix", p)
                for b in range(2):
                    o = 2 * IC * b
                    nc.scalar.copy(mix[o + IC:o + 2 * IC, :], src[o:o + IC, IS:2 * IS])
                    last = nc.scalar.copy(mix[o:o + IC, :], src[o + IC:o + 2 * IC, 0:IS])
                last.then_inc(sem("mix_ready"), 1)

                def joint(b, m, q):
                    use = f"joint{b}{q}{m}"
                    filled(act, use, k, p)
                    w = (QUART[q][1] - QUART[q][0]) * T
                    rows = (128, TAIL)[m]
                    nc.scalar.activation((j1, j2)[m][0:rows, b, cols(q)], bank(use, p)[0:rows, 0:w], ACT.Relu,
                                         bias=bggs[0:rows, m:m + 1]).then_inc(sem("joint_ready"), 1)

                def hidden(b, q):
                    filled(act, f"hid{b}{q}", k, p)
                    w = (QUART[q][1] - QUART[q][0]) * T
                    nc.scalar.activation(hid[:, b, cols(q)], bank(f"hid{b}{q}", p)[0:DS, 0:w], ACT.Relu,
                                         bias=bws1[:, :]).then_inc(sem("hid_ready"), 1)

                for m in range(2):
                    joint(0, m, 0)
                items(9, 10)
                for m in range(2):
                    joint(0, m, 1)
                items(10, 11)
                hidden(0, 0)
                for m in range(2):
                    joint(1, m, 0)
                items(11, 12)
                hidden(0, 1)
                for m in range(2):
                    joint(1, m, 1)
                items(12, 13)
                hidden(1, 0)
                items(13, 14)
                hidden(1, 1)
                items(14, 15)
                need(act, "szlogit_ready", k, p, 1)
                nc.scalar.activation(se[:, :], sz[:, :], ACT.Exp).then_inc(sem("sexp_ready"), 1)
                items(15, 16)
                need(act, "x1_ready", k, p, 1)
                nc.scalar.copy(x1h[:, :, :, :], x1[:, :, :, :]).then_inc(sem("x1_hi_ready"), 1)
                items(16, 19)
                for g in range(3):
                    if g:
                        items(18 + g, 19 + g)
                    filled(act, f"chan{g}", k, p)
                    src = bank(f"chan{g}", p)
                    for m in range(2 * g, min(2 * g + 2, MT)):
                        last = nc.scalar.activation(chan[:, m, :, :], src[:, 256 * (m % 2):256 * (m % 2) + 256]
                                                    .rearrange("p (b c) -> p b c", b=2), ACT.Relu, bias=bc[:, m:m + 1])
                    last.then_inc(sem("chan_ready"), 1)
                items(21, 22)
                filled(act, "gram", k, p)
                nc.scalar.copy(gram[:, :, :, :].rearrange("p a b c -> p (a b c)"), bank("gram", p)[:, :])\
                    .then_inc(sem("gram_ready"), 1)
                items(22, 23)
                filled(act, "jc", k, p)
                nc.scalar.activation(jc[:, :, :].rearrange("p b c -> p (b c)"), bank("jc", p)[0:IC, 0:256], ACT.Relu,
                                     bias=bggc[:, :]).then_inc(sem("jc_ready"), 1)
                items(23, 24)
                filled(act, "hc", k, p)
                nc.scalar.activation(hc[:, :, :].rearrange("p b c -> p (b c)"), bank("hc", p)[0:DC, 0:256], ACT.Relu,
                                     bias=bwc1[:, :]).then_inc(sem("hc_ready"), 1)
                items(24, 25)
                need(act, "czlogit_ready", k, p, 1)
                nc.scalar.activation(cz[:, 2, :], cz[:, 1, :], ACT.Exp).then_inc(sem("cexp_ready"), 1)
                items(25, 31)
                need(act, "rgap_ready", k, p, 1)
                nc.scalar.activation(mx[:, 3, :], mx[:, 2, :], ACT.Exp).then_inc(sem("rexp_ready"), 1)
                items(31, 32)
                for b in range(2):
                    filled(act, f"gates{b}", k, p)
                    src = bank(f"gates{b}", p)[:, :].bitcast(BF16)[0:KR, 0:S]
                    nc.scalar.copy(gt[p][:, b, :], src).then_inc(sem("gates_ready"), 1)

            units(act, step)
            experts(act, UNITS // 2, 0, 0, NEXP)

        @block.tensor
        def _(pe):
            pe.wait_ge(sem("ident_ready"), 3)
            pe.wait_ge(sem("rows_scaled"), 1)
            n = 0

            def prep_bank():
                if n >= NB:
                    if n - NB < 2 * NT:
                        pe.wait_ge(sem("prep_read"), n - NB + 1)
                    else:
                        pe.wait_ge(sem("wch_ready"), n - NB - 2 * NT + 1)
                        pe.wait_ge(sem("wcl_ready"), n - NB - 2 * NT + 1)
                return rot[n % NB]

            for j in range(NT):
                for m in range(2):
                    t = prep_bank()
                    nc.tensor.transpose(t[0:T, 0:98], raw_ggs[m][:, j * T:(j + 1) * T], ident[0:98, 0:98])
                    nc.tensor.transpose(t[0:T, 98:196], raw_ggs[m][:, S + j * T:S + (j + 1) * T], ident[0:98, 0:98])\
                        .then_inc(sem("prep_filled"), 1)
                    n += 1
            for m in range(MT):
                for j0, j1_ in QUART:
                    t = prep_bank()
                    for j in range(j0, j1_):
                        last = nc.tensor.transpose(t[0:T, (j - j0) * 128:(j - j0 + 1) * 128],
                                                   rawc_all[m][:, j * T:(j + 1) * T], ident[:, :])
                    last.then_inc(sem("prep_filled"), 1)
                    n += 1
            nc.tensor.transpose(gbank[0][0:C, 0:96], raw_w3[:, :], ident[0:96, 0:96])
            for i in range(2):
                nc.tensor.transpose(gbank[0][0:128, 128 + 64 * i:128 + 64 * i + DS], pad_ws1[:, 128 * i:128 * i + 128],
                                    ident[0:DS, 0:DS])
            for i in range(2):
                nc.tensor.transpose(gbank[0][0:C, 256 + 32 * i:288 + 32 * i], raw_ggc[:, i * C:(i + 1) * C],
                                    ident[0:IC, 0:IC])
            nc.tensor.transpose(gbank[0][0:IC, 320:320 + DC], raw_wc1[:, 1:1 + IC], ident[0:DC, 0:DC])
            for i in range(3):
                last = nc.tensor.transpose(gbank[0][0:128, 336 + 8 * i:336 + 8 * i + DC], pad_wc1[:, i, :],
                                           ident[0:DC, 0:DC])
            last.then_inc(sem("small_filled"), 1)
            pe.wait_ge(sem("weights_ready"), 1)
            pe.wait_ge(sem("wch_ready"), 2 * MT)
            pe.wait_ge(sem("wcl_ready"), 2 * MT)
            pe.wait_ge(sem("weh_ready"), 1)
            pe.wait_ge(sem("sel_ready"), 4)
            pe.wait_ge(sem("bias_stacked"), 16 * 9)
            pe.wait_ge(sem("cleared"), 4)

            def experts(pe, k, p, lo, hi):
                o = 1 - p
                for n in range(lo, hi):
                    if n < NEXP:
                        b, q = PIECES[n // E]
                        w = (QUART[q][1] - QUART[q][0]) * T
                        if n >= RING:
                            need(pe, "lo_ready", k, p, n + 1 - RING, back=1)
                        else:
                            need(pe, "lo_ready", k, p, NEXP + n + 1 - RING, back=2)
                        nc.tensor.matmul(gbank[n % RING][:, 0:w], selg[:, n % E, :], gt[o][:, b, cols(q)],
                                         start=True, stop=True).then_inc(sem("gate_seen"), 1)
                    m = n - LAG
                    if 0 <= m < NEXP:
                        b, q = PIECES[m // E]
                        e = m % E
                        w = (QUART[q][1] - QUART[q][0]) * T
                        if e == 0:
                            if m:
                                need(pe, "out_ready", k, p, m // E, back=1)
                            else:
                                need(pe, "out_ready", k, p, 4, back=2)
                            nc.tensor.matmul(acc[:, 0:w], bstk[:, :], gt[o][:, b, cols(q)], start=True, stop=False)
                        need(pe, "hi_ready", k, p, m + 1, back=1)
                        nc.tensor.matmul(acc[:, 0:w], weh[:, e, :], prod_h[:, m % RING, 0:w], start=False, stop=False)
                        nc.tensor.matmul(acc[:, 0:w], wel[:, e, :], prod_h[:, m % RING, 0:w], start=False, stop=False)
                        need(pe, "lo_ready", k, p, m + 1, back=1)
                        nc.tensor.matmul(acc[:, 0:w], weh[:, e, :], prod_l[:, m % RING, 0:w], start=False,
                                         stop=(e == E - 1)).then_inc(sem("exp_done"), 1)

            def step(pe, k, p):
                ex = not isinstance(k, int) or 2 * k + p > 0

                def items(lo, hi):
                    if ex:
                        experts(pe, k, p, lo, hi)

                def done(ins):
                    ins.then_inc(sem("bank_filled"), 1)

                pe.wait_ge(sem(f"x_loaded{p}"), (k + 1) * 16)
                for b, q in PIECES:
                    free(pe, f"x_tok{b}{q}", k, p)
                    for j in range(*QUART[q]):
                        last = nc.tensor.transpose(bank(f"x_tok{b}{q}", p)[0:T, (j - QUART[q][0]) * C:][:, 0:C],
                                                   x[p][:, b, j * T:(j + 1) * T], ident[:, :])
                    done(last)
                items(0, 3)
                for b, q in PIECES:
                    free(pe, f"y_ch{b}{q}", k, p)
                    need(pe, "y_tok_ready", k, p, 2 * b + q + 1)
                    for j in range(*QUART[q]):
                        last = nc.tensor.transpose(bank(f"y_ch{b}{q}", p)[:, (j - QUART[q][0]) * T:][:, 0:T],
                                                   y_tok[:, j, b, :], ident[0:T, 0:T])
                    done(last)
                items(3, 5)
                for b, q in PIECES:
                    free(pe, f"tp{b}{q}", k, p)
                    need(pe, "y_ch_ready", k, p, 2 * b + q + 1)
                    w = (QUART[q][1] - QUART[q][0]) * T
                    done(nc.tensor.matmul(bank(f"tp{b}{q}", p)[0:96, 0:w], w3[:, :], y_ch[:, b, cols(q)],
                                          start=True, stop=True))
                items(5, 7)
                for q in range(2):
                    free(pe, f"tp_tok{q}", k, p)
                    need(pe, "tp_ready", k, p, 3 + q)
                    for j in range(*QUART[q]):
                        last = nc.tensor.transpose(bank(f"tp_tok{q}", p)[0:T, (j - QUART[q][0]) * 128:][:, 0:128],
                                                   tp[:, j * T:(j + 1) * T], ident[:, :])
                    done(last)
                items(7, 9)
                free(pe, "mix", k, p)
                need(pe, "tp_tok_ready", k, p, 2)
                for j in range(NT):
                    last = nc.tensor.matmul(bank("mix", p)[:, 0:2 * IS], tp_tok[:, j, :],
                                            wggs[:, j, :], start=(j == 0), stop=(j == NT - 1))
                done(last)
                items(9, 10)

                def joint(b, q):
                    for m, (lo, hi) in enumerate(((0, 128), (128, IS))):
                        use = f"joint{b}{q}{m}"
                        free(pe, use, k, p)
                        need(pe, "mix_ready", k, p, 1)
                        w = (QUART[q][1] - QUART[q][0]) * T
                        done(nc.tensor.matmul(bank(use, p)[0:hi - lo, 0:w], mix[64 * b:64 * b + 64, lo:hi],
                                              tp[64 * b:64 * b + 64, cols(q)],
                                              start=True, stop=True))

                def hidden(b, q):
                    use = f"hid{b}{q}"
                    free(pe, use, k, p)
                    need(pe, "joint_ready", k, p, 4 * b + 2 * q + 2)
                    w = (QUART[q][1] - QUART[q][0]) * T
                    nc.tensor.matmul(bank(use, p)[0:DS, 0:w], wws1[:, 0, :], j1[:, b, cols(q)], start=True, stop=False)
                    done(nc.tensor.matmul(bank(use, p)[0:DS, 0:w], wws1[:, 1, :], j2[:, b, cols(q)],
                                          start=False, stop=True))

                joint(0, 0)
                items(10, 11)
                joint(0, 1)
                items(11, 12)
                hidden(0, 0)
                joint(1, 0)
                items(12, 13)
                hidden(0, 1)
                joint(1, 1)
                items(13, 14)
                hidden(1, 0)
                items(14, 15)
                hidden(1, 1)
                items(15, 16)
                free(pe, "slogit", k, p)
                for b in range(2):
                    need(pe, "hid_ready", k, p, 2 * b + 2)
                    for j in range(NT):
                        last = nc.tensor.matmul(bank("slogit", p)[0:T, NT * b + j:NT * b + j + 1],
                                                hid[:, b, j * T:(j + 1) * T], wws2[:, :], start=True, stop=True)
                done(last)
                items(16, 19)
                need(pe, "x1_hi_ready", k, p, 1)
                for g in range(3):
                    if g:
                        items(18 + g, 19 + g)
                    free(pe, f"chan{g}", k, p)
                    for m in range(2 * g, min(2 * g + 2, MT)):
                        o = bank(f"chan{g}", p)[:, 256 * (m % 2):256 * (m % 2) + 256]
                        mm = slice(m * 128, (m + 1) * 128)
                        for j in range(NT):
                            xh = x1h[:, j, :, :].rearrange("p b c -> p (b c)")
                            nc.tensor.matmul(o, wch[:, j, mm], xh, start=(j == 0), stop=False)
                            nc.tensor.matmul(o, wcl[:, j, mm], xh, start=False, stop=False)
                        if m == 0:
                            need(pe, "x1_lo_ready", k, p, 1)
                        for j in range(NT):
                            last = nc.tensor.matmul(o, wch[:, j, mm], x1l[:, j, :, :].rearrange("p b c -> p (b c)"),
                                                    start=False, stop=(j == NT - 1))
                    done(last)
                items(21, 22)
                free(pe, "gram", k, p)
                need(pe, "chan_ready", k, p, 2)
                for way in range(2):
                    for b in range(2):
                        o = bank("gram", p)[:, 256 * way + 128 * b:256 * way + 128 * b + 128]
                        for i, rows in ((0, 128), (2, TAIL)):
                            last = nc.tensor.matmul(o, chan[0:rows, i + way, b, :], chan[0:rows, i + 1 - way, b, :],
                                                    start=(i == 0), stop=(i == 2))
                done(last)
                items(22, 23)
                free(pe, "jc", k, p)
                need(pe, "gram_ready", k, p, 1)
                for way in range(2):
                    last = nc.tensor.matmul(bank("jc", p)[0:IC, 0:256], wggc[:, way, :],
                                            gram[:, 1 - way, :, :].rearrange("p b c -> p (b c)"),
                                            start=(way == 0), stop=(way == 1))
                done(last)
                items(23, 24)
                free(pe, "hc", k, p)
                need(pe, "jc_ready", k, p, 1)
                need(pe, "chan_ready", k, p, 3)
                o = bank("hc", p)[0:DC, 0:256]
                for i, rows in ((2, 128), (3, 128), (4, GX5)):
                    nc.tensor.matmul(o, wwc1g[0:rows, i - 2, :], chan[0:rows, i, :, :].rearrange("p b c -> p (b c)"),
                                     start=(i == 2), stop=False)
                done(nc.tensor.matmul(o, wwc1[:, :], jc[:, :, :].rearrange("p b c -> p (b c)"), start=False, stop=True))
                items(24, 25)
                free(pe, "clogit", k, p)
                need(pe, "hc_ready", k, p, 1)
                for b in range(2):
                    last = nc.tensor.matmul(bank("clogit", p)[:, b:b + 1], hc[:, b, :], wwc2[:, :], start=True, stop=True)
                done(last)
                items(25, 26)
                for b, q in PIECES:
                    free(pe, f"x1_ch{b}{q}", k, p)
                    for j in range(*QUART[q]):
                        last = nc.tensor.transpose(bank(f"x1_ch{b}{q}", p)[:, (j - QUART[q][0]) * T:][:, 0:T],
                                                   x1[:, j, b, :], ident[0:T, 0:T])
                    done(last)
                items(26, 28)
                for b, q in PIECES:
                    free(pe, f"x2_tok{b}{q}", k, p)
                    need(pe, "x2_ready", k, p, 2 * b + q + 1)
                    for j in range(*QUART[q]):
                        last = nc.tensor.transpose(bank(f"x2_tok{b}{q}", p)[0:T, (j - QUART[q][0]) * C:][:, 0:C],
                                                   x2[p][:, b, j * T:(j + 1) * T], ident[:, :])
                    done(last)
                items(28, 30)
                need(pe, "mean2_ready", k, p, 1)
                for b, q in PIECES:
                    free(pe, f"mean{b}{q}", k, p)
                    for j in range(*QUART[q]):
                        i = NT * b + j
                        last = nc.tensor.transpose(bank(f"mean{b}{q}", p)[:, (j - QUART[q][0]) * T:][:, 0:T],
                                                   mean2[:, i:i + 1].to_broadcast([T, 128]), ident[0:T, 0:T])
                    done(last)
                items(30, 31)
                free(pe, "rlogit", k, p)
                for b in range(2):
                    need(pe, "centred_ready", k, p, 2 * b + 2)
                    for j in range(NT):
                        i = NT * b + j
                        last = nc.tensor.matmul(bank("rlogit", p)[0:T, E * i:E * i + E], cen[p][:, b, j * T:(j + 1) * T],
                                                wr[:, :], start=True, stop=True)
                done(last)
                items(31, NEXP + LAG + 1)
                need(pe, "part", k, p, PER["part"])
                for b in range(2):
                    free(pe, f"gates{b}", k, p)
                    for j in range(NT):
                        last = nc.tensor.transpose(bank(f"gates{b}", p)[:, :].bitcast(BF16)[0:KR, j * T:(j + 1) * T],
                                                   gs[:, NT * b + j, :, :, :].rearrange("p i k e -> p (i k e)"),
                                                   identb[0:T, 0:T])
                    done(last)

            units(pe, step)
            need(pe, "gates_ready", UNITS // 2, 0, 2, back=1)
            experts(pe, UNITS // 2, 0, 0, NEXP + LAG + 1)

        @block.vector
        def _(dve):
            dve.wait_ge(sem("weights_loaded"), 16 * len(small))
            for m in range(2):
                nc.vector.tensor_scalar(raw_ggs[m], raw_ggs[m], raw_sggs[:, m:m + 1], None, ALU.mult)
            for m in range(MT):
                nc.vector.tensor_scalar(rawc_all[m], rawc_all[m], raw_sc[:, m:m + 1], None, ALU.mult)
            nc.vector.tensor_scalar(raw_w3[:, :], raw_w3[:, :], raw_s3[:, :], None, ALU.mult)
            nc.vector.memset(pad_ws1[:, :], 0.0)
            nc.vector.memset(pad_wc1[:, :, :], 0.0)
            nc.vector.tensor_scalar(raw_ws1[:, :], raw_ws1[:, :], raw_sws1[:, :], None, ALU.mult)
            nc.vector.tensor_scalar(raw_ggc[:, :], raw_ggc[:, :], raw_sggc[:, :], None, ALU.mult)
            nc.vector.tensor_scalar(raw_wc1[:, :], raw_wc1[:, :], raw_swc1[:, :], None, ALU.mult)\
                .then_inc(sem("prep_step"), 1)
            dve.wait_ge(sem("prep_step"), 1)
            nc.vector.tensor_copy(pad_ws1[:, 0:IS], raw_ws1[:, 1:1 + IS])
            nc.vector.tensor_scalar(pad_ws1[:, 224:256], raw_ws1[:, 0:1].to_broadcast([DS, IC]), 1.0 / IC, None,
                                    ALU.mult)
            for i, (lo, hi) in enumerate(((TAIL, 128), (TAIL, 128), (0, GX5))):
                last = nc.vector.tensor_scalar(pad_wc1[:, i, lo:hi], raw_wc1[:, 0:1].to_broadcast([DC, hi - lo]),
                                               1.0 / IS, None, ALU.mult)
            last.then_inc(sem("rows_scaled"), 1)
            nc.vector.tensor_scalar(sbs[:, :], raw_sbs[:, :], -1.0, None, ALU.mult)
            nc.vector.tensor_scalar(sbc[:, :], raw_sbc[:, :], -1.0, None, ALU.mult)
            for e in range(E):
                nc.vector.memset(pref[:, e:e + 1], float(E - e))
            nc.vector.tensor_copy(eb[:, 0, :], raw_eb[:, :]).then_inc(sem("bias_parts_ready"), 1)
            dve.wait_ge(sem("bias_parts_ready"), 1)
            nc.vector.tensor_tensor(res_eb[:, :], raw_eb[:, :], eb[:, 0, :], ALU.subtract).then_inc(sem("prep_step"), 1)
            dve.wait_ge(sem("prep_step"), 2)
            nc.vector.tensor_copy(eb[:, 1, :], res_eb[:, :]).then_inc(sem("bias_parts_ready"), 1)
            dve.wait_ge(sem("bias_parts_ready"), 2)
            nc.vector.tensor_tensor(raw_eb[:, :], res_eb[:, :], eb[:, 1, :], ALU.subtract).then_inc(sem("prep_step"), 1)
            dve.wait_ge(sem("prep_step"), 3)
            nc.vector.tensor_copy(eb[:, 2, :], raw_eb[:, :]).then_inc(sem("bias_parts_ready"), 1)
            n = 0
            for m in range(MT):
                for j0, j1_ in QUART:
                    dve.wait_ge(sem("wch_ready"), n + 1)
                    dst = slice(m * 128, (m + 1) * 128)
                    src = rot[(2 * NT + n) % NB][0:T, 0:(j1_ - j0) * 128].rearrange("p (j c) -> p j c", c=128)
                    nc.vector.tensor_tensor(wcl[:, j0:j1_, dst], src, wch[:, j0:j1_, dst].bitcast(F32), ALU.subtract)\
                        .then_inc(sem("wcl_ready"), 1)
                    n += 1
            dve.wait_ge(sem("small_filled"), 1)
            g = gbank[0]
            nc.vector.tensor_copy(w3[:, :], g[:, 0:96])
            nc.vector.tensor_copy(wws1[:, :, :], g[:, 128:256].rearrange("p (i c) -> p i c", i=2)[:, :, 0:DS])
            nc.vector.tensor_copy(wggc[:, :, :], g[:, 256:320].rearrange("p (i c) -> p i c", i=2))
            nc.vector.tensor_copy(wwc1[:, :], g[0:IC, 320:320 + DC])
            nc.vector.tensor_copy(wwc1g[:, :, :], g[:, 336:360].rearrange("p (i c) -> p i c", i=3))
            dve.wait_ge(sem("weh_ready"), 1)
            nc.vector.tensor_tensor(wel[:, :, :], raw_we, weh[:, :, :].bitcast(F32), ALU.subtract)\
                .then_inc(sem("weights_ready"), 1)
            dve.wait_ge(sem("weights_ready"), 1)

            def experts(dve, k, p, lo, hi):
                o = 1 - p
                for n in range(lo, hi):
                    if n % E == LAG and n > E:
                        c = n // E - 1
                        b, q = PIECES[c]
                        w = (QUART[q][1] - QUART[q][0]) * T
                        need(dve, "exp_done", k, p, E * (c + 1), back=1)
                        nc.vector.tensor_tensor(x2[o][:, b, cols(q)], acc[:, 0:w], x2[o][:, b, cols(q)], ALU.add)\
                            .then_inc(sem("out_ready"), 1)
                    if n < NEXP:
                        b, q = PIECES[n // E]
                        w = (QUART[q][1] - QUART[q][0]) * T
                        need(dve, "gate_seen", k, p, n + 1, back=1)
                        nc.vector.tensor_tensor(gbank[n % RING][:, 0:w], gbank[n % RING][:, 0:w],
                                                cen[o][:, b, cols(q)], ALU.mult).then_inc(sem("prod_ready"), 1)
                    m = n - 1
                    if 0 <= m < NEXP:
                        w = (QUART[(m // E) % 2][1] - QUART[(m // E) % 2][0]) * T
                        need(dve, "hi_ready", k, p, m + 1, back=1)
                        nc.vector.tensor_tensor(prod_l[:, m % RING, 0:w], gbank[m % RING][:, 0:w],
                                                prod_h[:, m % RING, 0:w].bitcast(F32), ALU.subtract)\
                            .then_inc(sem("lo_ready"), 1)

            def step(dve, k, p):
                ex = not isinstance(k, int) or 2 * k + p > 0
                small_steps = [0]

                def items(lo, hi):
                    if ex:
                        experts(dve, k, p, lo, hi)

                def then(ins, name="stat"):
                    small_steps[0] += 1
                    ins.then_inc(sem(name), 1)
                    need(dve, name, k, p, small_steps[0])

                def moments(mean, var, eps, ready):
                    me, mo, ve, vo = st[:, :, 1], st[:, :, 4], st[:, :, 2], st[:, :, 5]
                    nc.vector.tensor_tensor(sm[:, 0, :], me, mo, ALU.subtract).then_inc(sem("stat"), 1)
                    nc.vector.tensor_tensor(sm[:, 1, :], ve, vo, ALU.add).then_inc(sem("stat"), 1)
                    nc.vector.tensor_tensor(sm[:, 2, :], me, mo, ALU.add).then_inc(sem("stat"), 1)
                    small_steps[0] += 3
                    need(dve, "stat", k, p, small_steps[0])
                    then(nc.vector.tensor_tensor(sm[:, 3, :], sm[:, 0, :], sm[:, 0, :], ALU.mult))
                    then(nc.vector.scalar_tensor_tensor(out=sm[:, 4, :], in0=sm[:, 3, :], scalar=C / 4.0,
                                                        in1=sm[:, 1, :], op0=ALU.mult, op1=ALU.add))
                    then(nc.vector.tensor_scalar(mean[:, :], sm[:, 2, :], 0.5, None, ALU.mult))
                    nc.vector.tensor_scalar(var[:, :], sm[:, 4, :], 1.0 / C, eps, ALU.mult, ALU.add)\
                        .then_inc(sem(ready), 1)

                def tile_stats(kind):
                    for b, q in PIECES:
                        filled(dve, f"{kind}{b}{q}", k, p)
                        for j in range(*QUART[q]):
                            last = nc.vector.bn_stats(st[:, NT * b + j, :],
                                                      bank(f"{kind}{b}{q}", p)[0:T, (j - QUART[q][0]) * C:][:, 0:C])
                        last.then_inc(sem("stats2_ready" if kind == "x2_tok" else "tile_stats"), 1)

                PER["tile_stats"] = 4
                tile_stats("x_tok")
                need(dve, "tile_stats", k, p, 4)
                moments(mean1, var1, EPS1, "stats1_ready")
                items(0, 2)
                need(dve, "rstd1_ready", k, p, 1)
                for b, q in PIECES:
                    for j in range(*QUART[q]):
                        i = NT * b + j
                        last = nc.vector.tensor_scalar(y_tok[:, j, b, :],
                                                       bank(f"x_tok{b}{q}", p)[0:T, (j - QUART[q][0]) * C:][:, 0:C],
                                                       mean1[:, i:i + 1], rstd1[:, i:i + 1], ALU.subtract, ALU.mult)
                    last.then_inc(sem("y_tok_ready"), 1)
                items(2, 16)
                filled(dve, "slogit", k, p)
                nc.vector.tensor_scalar(sp1[:, :], bank("slogit", p)[0:T, 0:2 * NT], sbs[:, 0:1], sbs[:, 1:2],
                                        ALU.mult, ALU.add).then_inc(sem("slogit_read"), 1)
                need(dve, "slogit_read", k, p, 1)
                nc.vector.tensor_scalar(sz[:, :], sp1[:, :], 85.0, None, ALU.min).then_inc(sem("szlogit_ready"), 1)
                need(dve, "sexp_ready", k, p, 1)
                nc.vector.tensor_scalar(sp1[:, :], se[:, :], 1.0, None, ALU.add).then_inc(sem("sgate"), 1)
                need(dve, "sgate", k, p, 1)
                nc.vector.reciprocal(sig[:, :], sp1[:, :]).then_inc(sem("sgate"), 1)
                need(dve, "sgate", k, p, 2)
                for j in range(NT):
                    for b in range(2):
                        i = NT * b + j
                        last = nc.vector.tensor_scalar(x1[:, j, b, :], y_tok[:, j, b, :], sig[:, i:i + 1], None,
                                                       ALU.mult)
                last.then_inc(sem("x1_ready"), 1)
                items(16, 25)
                filled(dve, "clogit", k, p)
                nc.vector.tensor_scalar(cz[:, 0, :], bank("clogit", p)[:, 0:2], sbc[:, 0:1], sbc[:, 1:2],
                                        ALU.mult, ALU.add).then_inc(sem("clogit_read"), 1)
                need(dve, "clogit_read", k, p, 1)
                nc.vector.tensor_scalar(cz[:, 1, :], cz[:, 0, :], 85.0, None, ALU.min).then_inc(sem("czlogit_ready"), 1)
                need(dve, "cexp_ready", k, p, 1)
                nc.vector.tensor_scalar(cz[:, 3, :], cz[:, 2, :], 1.0, None, ALU.add).then_inc(sem("cgate"), 1)
                need(dve, "cgate", k, p, 1)
                nc.vector.reciprocal(cg[:, :], cz[:, 3, :]).then_inc(sem("cgate"), 1)
                need(dve, "cgate", k, p, 2)
                items(25, 26)
                if not isinstance(k, int) or k > 0:
                    dve.wait_ge(sem(f"stored{p}"), k * (16 * PAIR))
                for b, q in PIECES:
                    filled(dve, f"x1_ch{b}{q}", k, p)
                    w = (QUART[q][1] - QUART[q][0]) * T
                    nc.vector.scalar_tensor_tensor(out=x2[p][:, b, cols(q)], in0=bank(f"x1_ch{b}{q}", p)[:, 0:w],
                                                   scalar=cg[:, b:b + 1], in1=x[p][:, b, cols(q)],
                                                   op0=ALU.mult, op1=ALU.add).then_inc(sem("x2_ready"), 1)
                items(26, 28)
                tile_stats("x2_tok")
                need(dve, "stats2_ready", k, p, 4)
                moments(mean2, var2, EPS2, "mean2_ready")
                assert small_steps[0] == PER["stat"]
                items(28, 30)
                for b, q in PIECES:
                    filled(dve, f"mean{b}{q}", k, p)
                    w = (QUART[q][1] - QUART[q][0]) * T
                    nc.vector.tensor_tensor(cen[p][:, b, cols(q)], x2[p][:, b, cols(q)],
                                            bank(f"mean{b}{q}", p)[:, 0:w], ALU.subtract)\
                        .then_inc(sem("centred_ready"), 1)
                items(30, 31)

                def tiles(v):
                    return v.unsqueeze(2).to_broadcast([T, 2 * NT, E])

                def each(v):
                    return v.unsqueeze(1).to_broadcast([T, 2 * NT, E])

                small_steps[0] = 0

                def route(ins):
                    then(ins, "route")

                need(dve, "rstd2_ready", k, p, 1)
                filled(dve, "rlogit", k, p)
                src = bank("rlogit", p)[0:T, 0:2 * NT * E].rearrange("p (i e) -> p i e", e=E)
                nc.vector.tensor_tensor(lg[:, :, :], src, tiles(rstd2[:, :]), ALU.mult).then_inc(sem("rlogit_read"), 1)
                need(dve, "rlogit_read", k, p, 1)
                route(nc.vector.tensor_tensor(lg[:, :, :], lg[:, :, :], each(rb[:, :]), ALU.add))

                def pick(logits, top, hot):
                    route(nc.vector.tensor_tensor(eq[:, :, :], logits[:, :, :], tiles(top), ALU.is_equal))
                    route(nc.vector.tensor_tensor(eq[:, :, :], eq[:, :, :], each(pref[:, :]), ALU.mult))
                    route(nc.vector.tensor_reduce(mx[:, 4, :], eq[:, :, :], AX_X, ALU.max))
                    route(nc.vector.tensor_tensor(hot[:, :, :], eq[:, :, :], tiles(mx[:, 4, :]), ALU.is_equal))

                route(nc.vector.tensor_reduce(mx[:, 0, :], lg[:, :, :], AX_X, ALU.max))
                pick(lg, mx[:, 0, :], first)
                route(nc.vector.scalar_tensor_tensor(out=lg2[:, :, :].rearrange("p i e -> p (i e)"),
                                                     in0=first[:, :, :].rearrange("p i e -> p (i e)"), scalar=-BIG,
                                                     in1=lg[:, :, :].rearrange("p i e -> p (i e)"),
                                                     op0=ALU.mult, op1=ALU.add))
                route(nc.vector.tensor_reduce(mx[:, 1, :], lg2[:, :, :], AX_X, ALU.max))
                nc.vector.tensor_tensor(mx[:, 2, :], mx[:, 1, :], mx[:, 0, :], ALU.subtract)\
                    .then_inc(sem("rgap_ready"), 1)
                pick(lg2, mx[:, 1, :], second)
                need(dve, "rexp_ready", k, p, 1)
                route(nc.vector.tensor_scalar(mx[:, 5, :], mx[:, 3, :], 1.0, None, ALU.add))
                route(nc.vector.reciprocal(mx[:, 6, :], mx[:, 5, :]))
                route(nc.vector.tensor_tensor(mx[:, 7, :], mx[:, 6, :], mx[:, 3, :], ALU.mult))
                route(nc.vector.tensor_tensor(first[:, :, :], first[:, :, :], tiles(mx[:, 6, :]), ALU.mult))
                route(nc.vector.tensor_tensor(second[:, :, :], second[:, :, :], tiles(mx[:, 7, :]), ALU.mult))
                route(nc.vector.tensor_tensor(gv[:, :, 1, :], first[:, :, :], second[:, :, :], ALU.add))
                nc.vector.tensor_tensor(gv[:, :, 0, :], gv[:, :, 1, :], tiles(rstd2[:, :]), ALU.mult)\
                    .then_inc(sem("gatev_ready"), 1)
                assert small_steps[0] == ROUTE, small_steps[0]
                items(31, NEXP + LAG + 1)

            ROUTE = PER["route"] = 18
            units(dve, step)
            experts(dve, UNITS // 2, 0, 0, NEXP + LAG + 1)


_CONV = [f"{n}_{k}" for n in ("th", "ph", "ggs", "gxs", "ws1", "ws2", "thc", "phc", "ggc", "gxc", "wc1", "wc2")
         for k in ("w", "s", "b")]
_INS = {"x": "x"}
_INS.update({n: "L0_conv_" + n for n in _CONV})
_INS.update({n: "L0_ffn_" + n for n in ("router_w", "router_b", "expert_w", "expert_b")})


def kernel(**inputs):
    import numpy as _np
    import concourse.bacc as _bacc
    from concourse import mybir as _mybir
    from concourse.bass_utils import run_bass_kernel_spmd as _run

    nc = _bacc.Bacc("TRN2", target_bir_lowering=False, num_devices=1)
    arrays, args = {}, {}
    for short, name in _INS.items():
        v = _np.ascontiguousarray(inputs[name])
        arrays[f"in_{short}"] = v
        args[short] = nc.dram_tensor(f"in_{short}", v.shape, _mybir.dt.from_np(v.dtype), kind="ExternalInput").ap()
    o = nc.dram_tensor("out_0", (BATCH, C, HH, WW), _mybir.dt.float32, kind="ExternalOutput").ap()
    metaformer_kernel(nc, args, o)
    r = _run(nc, [arrays], core_ids=[0])
    return r.results[0]["out_0"]
```

```python
from contextlib import ExitStack

import concourse.bass as bass
from concourse import mybir

ALU = mybir.AluOpType
ACT = mybir.ActivationFunctionType
F32 = mybir.dt.float32
F32R = mybir.dt.float32r
BF16 = mybir.dt.bfloat16
AX_X = mybir.AxisListType.X

BATCH, C, HH, WW = 64, 128, 28, 28
S = HH * WW
T, NT = 112, 7
IC, IS = C // 4, S // 4
DS, DC = (1 + IS) // 4, (1 + IC) // 4
E = 8
PAIR = 2
UNITS = BATCH // PAIR
QUART = ((0, 4), (4, 7))
TAIL = IS - C
GX3, GX4 = C - TAIL, C - TAIL
GX5 = IS - GX3 - GX4
MT = 5
KR = 12 * E
EPS1, EPS2 = 1e-6, 1e-5
BIG = 1e30

PIECES = [(b, q) for b in range(2) for q in range(2)]

BACK = {"front": -1, "core": 0, "route": 1}
USES = (
    [(f"x2_tok{b}{q}", "route", "stats2_ready", 2 * b + q + 1) for b, q in PIECES]
    + [(f"tp{b}{q}", "core", "tp_ready", 2 * b + q + 1) for b, q in PIECES]
    + [(f"tp_tok{q}", "core", "tp_tok_ready", q + 1) for q in range(2)]
    + [(f"mean{b}{q}", "route", "centred_ready", 2 * b + q + 1) for b, q in PIECES]
    + [("mix", "core", "mix_ready", 1)]
    + [("rlogit", "route", "rlogit_read", 1)]
    + [(f"joint{b}0{m}", "core", "joint_ready", 2 * b + m + 1) for b in range(2) for m in range(2)]
    + [(f"x_tok0{q}", "front", "xt_ready", q + 1) for q in range(2)]
    + [(f"joint{b}1{m}", "core", "joint_ready", 4 + 2 * b + m + 1) for b in range(2) for m in range(2)]
    + [(f"hid{q}", "core", "hid_ready", q + 1) for q in range(2)]
    + [(f"x_tok1{q}", "front", "xt_ready", q + 3) for q in range(2)]
    + [("slogit", "core", "slogit_read", 1)]
    + [(f"gates{b}", "route", "gates_ready", b + 1) for b in range(2)]
    + [(f"chan{m}", "core", "chan_ready", m + 1) for m in range(3)]
    + [("gram", "core", "gram_ready", 1)]
    + [("y_ch00", "front", "y_ch_ready", 1), ("y_ch01", "front", "y_ch_ready", 2)]
    + [("jc", "core", "jc_ready", 1), ("y_ch10", "front", "y_ch_ready", 3)]
    + [("hc", "core", "hc_ready", 1), ("y_ch11", "front", "y_ch_ready", 4)]
    + [("clogit", "core", "clogit_read", 1)]
    + [(f"x1_ch{b}{q}", "core", "x2_ready", 2 * b + q + 1) for b, q in PIECES]
)
INDEX = {u[0]: n for n, u in enumerate(USES)}
NU = len(USES)
NB = 3
assert (2 * NU) % NB == 0
PER = {f"{stage}_filled": sum(u[1] == stage for u in USES) for stage in BACK}
NTH = {u[0]: sum(w[1] == u[1] for w in USES[:n + 1]) for n, u in enumerate(USES)}
for _name, _stage, _sem, _k in USES:
    PER[_sem] = max(PER.get(_sem, 0), _k)
NEXP = 4 * E
LAG = 4
RING = 4
STAT, ROUTE, PART = 6, 18, 8
PER.update(tp_hi_ready=4, tp_lo_ready=4, mix_hi_ready=2, mix_lo_ready=2,
           stat1=STAT, stat2=STAT, stats1_ready=1, y_tok_ready=4, rstd1_ready=1, rstd2_ready=1,
           mean2_ready=1, szlogit_ready=1, sexp_ready=1, x1_ready=2, x1_hi_ready=2, x1_lo_ready=2,
           czlogit_ready=1, cexp_ready=1, cgate=2, sgate=2, rgap_ready=1, rexp_ready=1, gatev_ready=1,
           route=ROUTE, part=PART, stats1_read=2,
           gate_seen=NEXP, prod_ready=NEXP, hi_ready=NEXP, lo_ready=NEXP // 2, lo_pool_ready=NEXP // 2,
           exp_done=NEXP, out_ready=4)


def width(n):
    q = (n // E) % 2
    return (QUART[q][1] - QUART[q][0]) * T


def cols(q):
    return slice(QUART[q][0] * T, QUART[q][1] * T)


def metaformer_kernel(nc, a, out):
    with ExitStack() as ctx:
        def sb(name, shape, dt=F32):
            return ctx.enter_context(nc.sbuf_tensor(name, shape, dt))

        sems = {}

        def sem(name):
            if name not in sems:
                sems[name] = ctx.enter_context(nc.semaphore(name))
            return sems[name]

        rot = [ctx.enter_context(nc.psum_tensor(f"rot{i}", [128, 512], F32)) for i in range(NB)]
        gbank = [ctx.enter_context(nc.psum_tensor(f"gbank{i}", [128, 512], F32)) for i in range(3)]
        acc = [ctx.enter_context(nc.psum_tensor(f"acc{i}", [128, 512], F32)) for i in range(2)]

        ident = sb("ident", [128, 128])
        identb = sb("identb", [128, 128], BF16)
        w3 = sb("w3", [C, 3 * IC])
        b3 = sb("b3", [3 * IC, 1])
        wggs = sb("wggs", [T, NT, 2 * IS])
        bggs = sb("bggs", [128, 2])
        wws1 = sb("wws1", [128, 2, 64])
        bws1 = sb("bws1", [128, 1])
        wws2 = sb("wws2", [128, 2])
        sbs = sb("sbs", [T, 2])
        wch = sb("wch", [T, NT, MT * 128], F32R)
        wcl = sb("wcl", [T, NT, MT * 128], F32R)
        bc = sb("bc", [128, MT])
        wggc = sb("wggc", [C, 2, IC])
        bggc = sb("bggc", [IC, 1])
        wwc1 = sb("wwc1", [IC, DC])
        wwc1g = sb("wwc1g", [128, 3, DC])
        bwc1 = sb("bwc1", [DC, 1])
        wwc2 = sb("wwc2", [DC, 1])
        sbc = sb("sbc", [C, 2])
        wr = sb("wr", [C, E])
        rb = sb("rb", [T, E])
        pref = sb("pref", [T, E])
        weh = sb("weh", [C, E, C], F32R)
        wel = sb("wel", [C, E, C], F32R)
        selg = sb("selg", [KR, E, 128], BF16)
        bstk = sb("bstk", [KR, C], BF16)
        one = sb("one", [T, 1])
        mhalf = sb("mhalf", [T, 2 * NT])

        x = [sb(f"xin{p}", [C, PAIR, S]) for p in range(2)]
        x2 = [sb(f"x2_{p}", [C, PAIR, S]) for p in range(2)]
        cen = [sb(f"cen{p}", [C, PAIR, S]) for p in range(2)]
        gt = [sb(f"gt{p}", [KR, PAIR, S], BF16) for p in range(2)]
        st = sb("st", [T, 2 * NT, 6])
        sm = sb("sm", [T, 5, 2 * NT])
        tok = [sb(f"tok{p}", [T, NT, PAIR, C]) for p in range(2)]
        mean1 = sb("mean1", [T, 2 * NT])
        var1 = sb("var1", [T, 2 * NT])
        rstd1 = sb("rstd1", [T, 2 * NT])
        mean2 = sb("mean2", [T, 2 * NT])
        var2 = sb("var2", [T, 2 * NT])
        rstd2 = sb("rstd2", [T, 2 * NT])
        y_ch = sb("y_ch", [C, PAIR, S])
        tp = sb("tp", [128, S])
        tp_h = [sb(f"tp_h{b}", [128, S], F32R) for b in range(2)]
        tp_l = sb("tp_l", [128, S], F32R)
        tp_tok = sb("tp_tok", [T, NT, 128])
        mix = sb("mix", [128, IS])
        mix_s = [sb(f"mix_s{b}", [128, IS], F32R) for b in range(2)]
        j1 = sb("j1", [128, PAIR, S])
        j2 = sb("j2", [128, PAIR, S])
        hid = sb("hid", [128, S])
        sz = sb("sz", [T, 2 * NT])
        se = sb("se", [T, 2 * NT])
        sp1 = sb("sp1", [T, 2 * NT])
        sig = sb("sig", [T, 2 * NT])
        x1h = sb("x1h", [T, NT, PAIR, C], F32R)
        x1l = sb("x1l", [T, NT, PAIR, C], F32R)
        chan = sb("chan", [128, MT, PAIR, C])
        gram = sb("gram", [C, 2, PAIR, C])
        jc = sb("jc", [IC, PAIR, C])
        hc = sb("hc", [DC, PAIR, C])
        cz = sb("cz", [C, 4, PAIR])
        cg = sb("cg", [C, PAIR])
        lg = sb("lg", [T, 2 * NT, E])
        lg2 = sb("lg2", [T, 2 * NT, E])
        eq = sb("eq", [T, 2 * NT, E])
        first = sb("first", [T, 2 * NT, E])
        second = sb("second", [T, 2 * NT, E])
        mx = sb("mx", [T, 8, 2 * NT])
        gv = sb("gv", [T, 2 * NT, 2, E])
        gs = sb("gs", [T, 2 * NT, 3, 4, E], BF16)
        prod = sb("prod", [C, 4, 448])
        prod_h = sb("prod_h", [C, RING, 448], F32R)
        prod_l = sb("prod_l", [C, RING, 448], F32R)

        block = ctx.enter_context(nc.Block())

        def live(k, p, back):
            return not isinstance(k, int) or 0 <= 2 * k + p - back < UNITS

        def need(eng, name, k, p, n, back=0):
            if isinstance(k, int) and 2 * k + p - back < 0:
                return
            eng.wait_ge(sem(name), k * (2 * PER[name]) + ((p - back) * PER[name] + n))

        def ago(i, d, back):
            return (i - d, back) if i >= d else (i - d + NEXP, back + 1)

        def bank(use, p):
            return rot[(p * NU + INDEX[use]) % NB]

        def free(eng, use, k, p):
            n = INDEX[use] - NB
            while True:
                _, stage, s, c = USES[n % NU]
                back = BACK[stage] - n // NU
                if live(k, p, back) or n < -2 * NU:
                    break
                n -= NB
            if live(k, p, back):
                need(eng, s, k, p, c, back=back)

        def filled(eng, use, k, p):
            stage = USES[INDEX[use]][1]
            need(eng, stage + "_filled", k, p, NTH[use], back=BACK[stage])

        def steps(eng, step):
            step(eng, -1, 1)
            step(eng, 0, 0)
            step(eng, 0, 1)
            with eng.Fori(1, UNITS // 2 - 1) as k:
                step(eng, k, 0)
                step(eng, k, 1)
            for k in range(UNITS // 2 - 1, UNITS // 2 + 1):
                step(eng, k, 0)
                step(eng, k, 1)

        rawc_all = [x2[0][:, 0, :], x2[0][:, 1, :], x2[1][:, 0, :], x2[1][:, 1, :], cen[0][:, 0, :]]
        raw_ggs = [cen[1][0:98, :, :].rearrange("p b s -> p (b s)"), y_ch[0:98, :, :].rearrange("p b s -> p (b s)")]
        spare = chan[:, :, :, :].rearrange("p m b c -> p (m b c)")
        raw_w3 = spare[0:3 * IC, 0:C]
        raw_s3 = sb("raw_s3", [3 * IC, 1])
        raw_sggs = sb("raw_sggs", [98, 2])
        raw_ws1 = spare[0:DS, C:C + 1 + IS]
        pad_ws1 = spare[0:DS, 3 * C:5 * C]
        raw_sws1 = sb("raw_sws1", [DS, 1])
        raw_sbs = sb("raw_sbs", [T, 2])
        raw_sc = sb("raw_sc", [128, MT])
        raw_ggc = spare[0:IC, 5 * C:7 * C]
        raw_sggc = sb("raw_sggc", [IC, 1])
        raw_wc1 = sb("raw_wc1", [DC, 1 + IC])
        pad_wc1 = spare[0:DC, 7 * C:10 * C].rearrange("p (t c) -> p t c", t=3)
        raw_swc1 = sb("raw_swc1", [DC, 1])
        raw_sbc = sb("raw_sbc", [C, 2])
        raw_we = j1[:, :, :].rearrange("p b s -> p (b s)")[:, 0:E * C].rearrange("p (e c) -> p e c", e=E)
        raw_eb = tp[0:E, 0:C]
        res_eb = tp[0:E, C:2 * C]
        eb = sb("eb", [E, 3, C], BF16)

        def col(v):
            return v.rearrange("(n o) -> n o", o=1)

        x_dram = a["x"].rearrange("n c h w -> n c (h w)")
        o_dram = out.rearrange("n c h w -> n c (h w)")

        small = [
            (raw_w3[0:32, :], a["th_w"]), (raw_w3[32:64, :], a["ph_w"]), (raw_w3[64:96, :], a["gxs_w"]),
            (raw_s3[0:32, :], col(a["th_s"])), (raw_s3[32:64, :], col(a["ph_s"])), (raw_s3[64:96, :], col(a["gxs_s"])),
            (b3[0:32, :], col(a["th_b"])), (b3[32:64, :], col(a["ph_b"])), (b3[64:96, :], col(a["gxs_b"])),
            (raw_ggs[0], a["ggs_w"][0:98, :]), (raw_ggs[1], a["ggs_w"][98:196, :]),
            (raw_sggs[:, 0:1], col(a["ggs_s"][0:98])), (raw_sggs[:, 1:2], col(a["ggs_s"][98:196])),
            (bggs[0:128, 0:1], col(a["ggs_b"][0:128])), (bggs[0:TAIL, 1:2], col(a["ggs_b"][128:196])),
            (raw_ws1[:, :], a["ws1_w"]), (raw_sws1[:, :], col(a["ws1_s"])), (bws1[0:DS, :], col(a["ws1_b"])),
            (bws1[64:64 + DS, :], col(a["ws1_b"])),
            (wws2[0:DS, 0:1], a["ws2_w"].rearrange("o n -> n o")),
            (wws2[64:64 + DS, 1:2], a["ws2_w"].rearrange("o n -> n o")),
            (raw_sbs[:, 0:1], a["ws2_s"].partition_broadcast(T)), (raw_sbs[:, 1:2], a["ws2_b"].partition_broadcast(T)),
            (raw_ggc[:, :], a["ggc_w"]), (raw_sggc[:, :], col(a["ggc_s"])), (bggc[:, :], col(a["ggc_b"])),
            (raw_wc1[:, :], a["wc1_w"]), (raw_swc1[:, :], col(a["wc1_s"])), (bwc1[:, :], col(a["wc1_b"])),
            (wwc2[:, :], a["wc2_w"].rearrange("o n -> n o")),
            (raw_sbc[:, 0:1], a["wc2_s"].partition_broadcast(C)), (raw_sbc[:, 1:2], a["wc2_b"].partition_broadcast(C)),
            (wr[:, :], a["router_w"]), (rb[:, :], a["router_b"].partition_broadcast(T)),
            (raw_we, a["expert_w"].rearrange("e d c -> d e c")), (raw_eb[:, :], a["expert_b"]),
        ]
        stack = [(0, 0, "thc", 0, 128), (1, 0, "phc", 0, 128), (2, 0, "thc", 128, IS), (3, 0, "phc", 128, IS),
                 (2, TAIL, "gxc", 0, GX3), (3, TAIL, "gxc", GX3, GX3 + GX4), (4, 0, "gxc", GX3 + GX4, IS)]
        for m, r, w, lo, hi in stack:
            small += [(rawc_all[m][r:r + hi - lo, :], a[w + "_w"][lo:hi, :]),
                      (raw_sc[r:r + hi - lo, m:m + 1], col(a[w + "_s"][lo:hi])),
                      (bc[r:r + hi - lo, m:m + 1], col(a[w + "_b"][lo:hi]))]

        def load_x(eng, k, p):
            u2 = (2 * k + p) * PAIR
            eng.dma_start(x[p][:, :, :], x_dram[bass.ds(u2, PAIR)].rearrange("b c s -> c b s"))\
               .then_inc(sem(f"x_loaded{p}"), 16)

        def store(eng, k, p, b):
            need(eng, "out_ready", k, p, 2 * b + 2, back=2)
            img = (2 * k + p - 2) * PAIR + b
            eng.dma_start(o_dram[bass.ds(img, 1)].rearrange("b c s -> c b s"), x2[p][:, b:b + 1, :])\
               .then_inc(sem(f"stored{p}"), 16)

        @block.sync
        def _(sp):
            load_x(sp, 0, 0)
            sp.wait_ge(sem("zeroed"), 5)
            for dst, src in small:
                sp.dma_start(dst, src).then_inc(sem("weights_loaded"), 16)
            load_x(sp, 0, 1)
            sp.wait_ge(sem("bias_parts_ready"), 3)
            sp.wait_ge(sem("cleared"), 4)
            for i in range(3):
                for j in range(3):
                    r = 4 * E * i + E * (1 + j)
                    sp.dma_start(bstk[r:r + E, :], eb[:, j, :]).then_inc(sem("bias_stacked"), 16)

            def step(sp, k, p):
                for b in range(2):
                    if live(k, p, 2):
                        store(sp, k, p, b)
                if live(k, p, 0) and live(k, p, -2):
                    need(sp, "x2_ready", k, p, 4)
                    load_x(sp, k + 1, p)

            steps(sp, step)
            for p in range(2):
                sp.wait_ge(sem(f"stored{p}"), 16 * PAIR * UNITS // 2)

        @block.gpsimd
        def _(pool):
            nc.gpsimd.memset(cen[0][:, 0, :], 0.0).then_inc(sem("zeroed"), 1)
            nc.gpsimd.memset(raw_sc[:, :], 0.0).then_inc(sem("zeroed"), 1)
            nc.gpsimd.memset(bc[:, :], 0.0).then_inc(sem("zeroed"), 1)
            nc.gpsimd.memset(bws1[:, :], 0.0).then_inc(sem("zeroed"), 1)
            nc.gpsimd.memset(wws2[:, :], 0.0).then_inc(sem("zeroed"), 1)
            nc.gpsimd.memset(bstk[:, :], 0.0).then_inc(sem("cleared"), 1)
            pool.wait_ge(sem("zeroed"), 5)
            pool.wait_ge(sem("cleared"), 1)
            nc.gpsimd.memset(j2[64:96, :, :], 0.0).then_inc(sem("cleared"), 1)
            pool.wait_ge(sem("cleared"), 2)
            nc.gpsimd.memset(one[:, :], 1.0).then_inc(sem("cleared"), 1)
            nc.gpsimd.memset(mhalf[:, :], -0.5).then_inc(sem("cleared"), 1)
            nc.gpsimd.memset(ident[:, :], 0.0).then_inc(sem("ident_ready"), 1)
            nc.gpsimd.memset(selg[:, :, :], 0.0).then_inc(sem("sel_ready"), 1)
            pool.wait_ge(sem("ident_ready"), 1)
            nc.gpsimd.affine_select(out=ident[:, :], in_=ident[:, :], compare_op=ALU.not_equal, fill=1.0,
                                    base=0, pattern=[[-1, 128]], channel_multiplier=1).then_inc(sem("ident_ready"), 1)
            pool.wait_ge(sem("ident_ready"), 2)
            nc.gpsimd.tensor_copy(identb[:, :], ident[:, :]).then_inc(sem("ident_ready"), 1)
            for i in range(3):
                pool.wait_ge(sem("sel_ready"), i + 1)
                nc.gpsimd.affine_select(out=selg[:, :, :], in_=selg[:, :, :], compare_op=ALU.not_equal, fill=1.0,
                                        base=-4 * E * i, pattern=[[-1, E], [0, 128]], channel_multiplier=1)\
                    .then_inc(sem("sel_ready"), 1)

            def experts(pool, k, p, back, lo, hi):
                for n in range(lo, hi):
                    m, mb = ago(n, 1, back)
                    if m % 2 and live(k, p, mb):
                        w = width(m)
                        need(pool, "hi_ready", k, p, m + 1, back=mb)
                        nc.gpsimd.tensor_tensor(prod_l[:, m % RING, 0:w], prod[:, (m // 2) % 4, 0:w],
                                                prod_h[:, m % RING, 0:w].bitcast(F32), ALU.subtract)\
                            .then_inc(sem("lo_pool_ready"), 1)

            def step(pool, k, p):
                core, front, route = live(k, p, 0), live(k, p, -1), live(k, p, 1)
                part = [0]

                def old(lo, hi):
                    experts(pool, k, p, 2, lo, hi)

                def new(lo, hi):
                    experts(pool, k, p, 1, lo, hi)

                def stacked(ins):
                    part[0] += 1
                    ins.then_inc(sem("part"), 1)

                def split_gates(i):
                    ones2 = one[:, :].unsqueeze(1).unsqueeze(1).to_broadcast([T, 2 * NT, 2, E])
                    stacked(nc.gpsimd.tensor_tensor(gs[:, :, i, 0:2, :], gv[:, :, :, :], ones2, ALU.mult))
                    need(pool, "part", k, p, part[0], back=1)
                    if i < 2:
                        stacked(nc.gpsimd.tensor_tensor(gv[:, :, :, :], gv[:, :, :, :], gs[:, :, i, 0:2, :],
                                                        ALU.subtract))
                    stacked(nc.gpsimd.tensor_tensor(gs[:, :, i, 2:4, :], gs[:, :, i, 1:2, :].to_broadcast([T, 2 * NT, 2, E]),
                                                    ones2, ALU.mult))
                    need(pool, "part", k, p, part[0], back=1)

                old(16, 20)
                if route:
                    need(pool, "mean2_ready", k, p, 1, back=1)
                    nc.gpsimd.tensor_tensor(rstd2[:, :], var2[:, :], mhalf[:, :], ALU.pow)\
                        .then_inc(sem("rstd2_ready"), 1)
                    need(pool, "rstd2_ready", k, p, 1, back=1)
                if core:
                    for q in range(2):
                        for b in range(2):
                            if q or b:
                                need(pool, "tp_lo_ready", k, p, 2 * q + b)
                            need(pool, "tp_hi_ready", k, p, 2 * q + b + 1)
                            rows = slice(64 * b, 64 * b + 64)
                            nc.gpsimd.tensor_tensor(tp_l[rows, cols(q)], tp[rows, cols(q)],
                                                    tp_h[b][rows, cols(q)].bitcast(F32), ALU.subtract)\
                                .then_inc(sem("tp_lo_ready"), 1)
                    need(pool, "tp_lo_ready", k, p, 4)
                old(20, 25)
                if route:
                    need(pool, "gatev_ready", k, p, 1, back=1)
                    split_gates(0)
                    split_gates(1)
                old(25, 27)
                if route:
                    split_gates(2)
                    assert part[0] == PART
                old(27, 29)
                if core:
                    for g, (lo, hi) in enumerate(QUART):
                        if g:
                            old(29, 31)
                        need(pool, "x1_hi_ready", k, p, g + 1)
                        nc.gpsimd.tensor_tensor(x1l[:, lo:hi, :, :], tok[p][:, lo:hi, :, :],
                                                x1h[:, lo:hi, :, :].bitcast(F32), ALU.subtract)\
                            .then_inc(sem("x1_lo_ready"), 1)
                else:
                    old(29, 31)
                old(31, 32)
                new(0, 1)
                if front:
                    need(pool, "stats1_ready", k, p, 1, back=-1)
                    nc.gpsimd.tensor_tensor(rstd1[:, :], var1[:, :], mhalf[:, :], ALU.pow)\
                        .then_inc(sem("rstd1_ready"), 1)
                new(1, 16)

            steps(pool, step)

        @block.scalar
        def _(act):
            n = 0
            for j in range(NT):
                for m in range(2):
                    act.wait_ge(sem("prep_filled"), n + 1)
                    half = rot[n % NB]
                    nc.scalar.copy(wggs[:, j, 98 * m:98 * m + 98], half[0:T, 0:98])
                    nc.scalar.copy(wggs[:, j, IS + 98 * m:IS + 98 * m + 98], half[0:T, 98:196])\
                        .then_inc(sem("prep_read"), 1)
                    n += 1
            for m in range(MT):
                for j0, j1_ in QUART:
                    act.wait_ge(sem("prep_filled"), n + 1)
                    src = rot[n % NB][0:T, 0:(j1_ - j0) * 128].rearrange("p (j c) -> p j c", c=128)
                    nc.scalar.copy(wch[:, j0:j1_, m * 128:(m + 1) * 128], src).then_inc(sem("wch_ready"), 1)
                    n += 1
            act.wait_ge(sem("weights_loaded"), 16 * len(small))
            nc.scalar.copy(weh[:, :, :], raw_we).then_inc(sem("weh_ready"), 1)

            def experts(act, k, p, back, lo, hi):
                for n in range(lo, hi):
                    if live(k, p, back):
                        w = width(n)
                        m, mb = ago(n, RING, back)
                        need(act, "exp_done", k, p, m + 1, back=mb)
                        need(act, "prod_ready", k, p, n + 1, back=back)
                        src = prod[:, (n // 2) % 4, 0:w] if n % 2 else gbank[(n // 2) % 2][:, 0:w]
                        nc.scalar.copy(prod_h[:, n % RING, 0:w], src).then_inc(sem("hi_ready"), 1)

            def step(act, k, p):
                core, front, route = live(k, p, 0), live(k, p, -1), live(k, p, 1)

                def old(lo, hi):
                    experts(act, k, p, 2, lo, hi)

                def new(lo, hi):
                    experts(act, k, p, 1, lo, hi)

                old(16, 17)
                if core:
                    for b, q in PIECES:
                        filled(act, f"tp{b}{q}", k, p)
                        src = bank(f"tp{b}{q}", p)
                        w = (QUART[q][1] - QUART[q][0]) * T
                        nc.scalar.activation(tp[64 * b:64 * b + 64, cols(q)], src[0:2 * IC, 0:w], ACT.Relu,
                                             bias=b3[0:2 * IC, :])
                        nc.scalar.activation(j2[96:128, b, cols(q)], src[2 * IC:3 * IC, 0:w], ACT.Relu,
                                             bias=b3[2 * IC:3 * IC, :]).then_inc(sem("tp_ready"), 1)
                        if (b, q) == (0, 1):
                            old(17, 18)
                else:
                    old(17, 18)
                old(18, 20)
                if core:
                    for q in range(2):
                        filled(act, f"tp_tok{q}", k, p)
                        j0, jn = QUART[q]
                        src = bank(f"tp_tok{q}", p)[0:T, 0:(jn - j0) * 128].rearrange("p (j c) -> p j c", c=128)
                        nc.scalar.copy(tp_tok[:, j0:jn, :], src).then_inc(sem("tp_tok_ready"), 1)
                    for q in range(2):
                        for b in range(2):
                            src = tp[64 * b:64 * b + 64, cols(q)]
                            nc.scalar.copy(tp_h[b][64 * b:64 * b + 64, cols(q)], src)
                            nc.scalar.copy(tp_h[b][64 - 64 * b:128 - 64 * b, cols(q)], src)\
                                .then_inc(sem("tp_hi_ready"), 1)
                old(20, 21)
                if core:
                    filled(act, "mix", k, p)
                    src = bank("mix", p)
                    for b in range(2):
                        o = 2 * IC * b
                        nc.scalar.copy(mix[o + IC:o + 2 * IC, :], src[o:o + IC, IS:2 * IS])
                        last = nc.scalar.copy(mix[o:o + IC, :], src[o + IC:o + 2 * IC, 0:IS])
                    last.then_inc(sem("mix_ready"), 1)
                    need(act, "mix_ready", k, p, 1)
                    for b in range(2):
                        nc.scalar.copy(mix_s[b][64 * b:64 * b + 64, :], mix[64 * b:64 * b + 64, :])\
                            .then_inc(sem("mix_hi_ready"), 1)
                old(21, 23)

                def joint(q):
                    for b in range(2):
                        for m in range(2):
                            use = f"joint{b}{q}{m}"
                            filled(act, use, k, p)
                            w = (QUART[q][1] - QUART[q][0]) * T
                            rows = (128, TAIL)[m]
                            nc.scalar.activation((j1, j2)[m][0:rows, b, cols(q)], bank(use, p)[0:rows, 0:w], ACT.Relu,
                                                 bias=bggs[0:rows, m:m + 1]).then_inc(sem("joint_ready"), 1)

                def hidden(q):
                    filled(act, f"hid{q}", k, p)
                    w = (QUART[q][1] - QUART[q][0]) * T
                    nc.scalar.activation(hid[:, cols(q)], bank(f"hid{q}", p)[:, 0:w], ACT.Relu,
                                         bias=bws1[:, :]).then_inc(sem("hid_ready"), 1)

                def router_exp():
                    need(act, "rgap_ready", k, p, 1, back=1)
                    nc.scalar.activation(mx[:, 3, :], mx[:, 2, :], ACT.Exp).then_inc(sem("rexp_ready"), 1)

                def x_tokens(b):
                    for q in range(2):
                        filled(act, f"x_tok{b}{q}", k, p)
                        j0, jn = QUART[q]
                        src = bank(f"x_tok{b}{q}", p)[0:T, 0:(jn - j0) * C].rearrange("p (j c) -> p j c", c=C)
                        nc.scalar.copy(tok[1 - p][:, j0:jn, b, :], src).then_inc(sem("xt_ready"), 1)

                if core:
                    joint(0)
                if front:
                    x_tokens(0)
                if route:
                    router_exp()
                old(23, 24)
                if core:
                    joint(1)
                old(24, 25)
                if core:
                    hidden(0)
                old(25, 26)
                if core:
                    hidden(1)
                if front:
                    x_tokens(1)
                if core:
                    need(act, "szlogit_ready", k, p, 1)
                    nc.scalar.activation(se[:, :], sz[:, :], ACT.Exp).then_inc(sem("sexp_ready"), 1)
                old(26, 27)
                if route:
                    for b in range(2):
                        filled(act, f"gates{b}", k, p)
                        src = bank(f"gates{b}", p)[:, :].bitcast(BF16)[0:KR, 0:S]
                        nc.scalar.copy(gt[1 - p][:, b, :], src).then_inc(sem("gates_ready"), 1)
                if core:
                    for g, (lo, hi) in enumerate(QUART):
                        need(act, "x1_ready", k, p, g + 1)
                        nc.scalar.copy(x1h[:, lo:hi, :, :], tok[p][:, lo:hi, :, :]).then_inc(sem("x1_hi_ready"), 1)
                        old(27 + 2 * g, 29 + 2 * g)
                else:
                    old(27, 31)
                old(31, 32)
                new(0, 1)

                def channels(g):
                    filled(act, f"chan{g}", k, p)
                    src = bank(f"chan{g}", p)
                    for m in range(2 * g, min(2 * g + 2, MT)):
                        last = nc.scalar.activation(chan[:, m, :, :], src[:, 256 * (m % 2):256 * (m % 2) + 256]
                                                    .rearrange("p (b c) -> p b c", b=2), ACT.Relu, bias=bc[:, m:m + 1])
                    last.then_inc(sem("chan_ready"), 1)

                def back_to_channels(b, q):
                    filled(act, f"y_ch{b}{q}", k, p)
                    w = (QUART[q][1] - QUART[q][0]) * T
                    nc.scalar.copy(y_ch[:, b, cols(q)], bank(f"y_ch{b}{q}", p)[:, 0:w]).then_inc(sem("y_ch_ready"), 1)

                new(1, 2)
                if core:
                    channels(0)
                new(2, 3)
                if core:
                    channels(1)
                new(3, 5)
                if core:
                    channels(2)
                new(5, 6)
                if core:
                    filled(act, "gram", k, p)
                    nc.scalar.copy(gram[:, :, :, :].rearrange("p a b c -> p (a b c)"), bank("gram", p)[:, :])\
                        .then_inc(sem("gram_ready"), 1)
                if front:
                    back_to_channels(0, 0)
                    back_to_channels(0, 1)
                new(6, 8)
                if core:
                    filled(act, "jc", k, p)
                    nc.scalar.activation(jc[:, :, :].rearrange("p b c -> p (b c)"), bank("jc", p)[0:IC, 0:256],
                                         ACT.Relu, bias=bggc[:, :]).then_inc(sem("jc_ready"), 1)
                if front:
                    back_to_channels(1, 0)
                new(8, 9)
                if core:
                    filled(act, "hc", k, p)
                    nc.scalar.activation(hc[:, :, :].rearrange("p b c -> p (b c)"), bank("hc", p)[0:DC, 0:256],
                                         ACT.Relu, bias=bwc1[:, :]).then_inc(sem("hc_ready"), 1)
                if front:
                    back_to_channels(1, 1)
                new(9, 11)
                if core:
                    need(act, "czlogit_ready", k, p, 1)
                    nc.scalar.activation(cz[:, 2, :], cz[:, 1, :], ACT.Exp).then_inc(sem("cexp_ready"), 1)
                new(11, 16)

            steps(act, step)

        @block.tensor
        def _(pe):
            pe.wait_ge(sem("ident_ready"), 3)
            pe.wait_ge(sem("rows_scaled"), 1)
            n = 0

            def prep_bank():
                if n >= NB:
                    if n - NB < 2 * NT:
                        pe.wait_ge(sem("prep_read"), n - NB + 1)
                    else:
                        pe.wait_ge(sem("wch_ready"), n - NB - 2 * NT + 1)
                        pe.wait_ge(sem("wcl_ready"), n - NB - 2 * NT + 1)
                return rot[n % NB]

            for j in range(NT):
                for m in range(2):
                    t = prep_bank()
                    nc.tensor.transpose(t[0:T, 0:98], raw_ggs[m][:, j * T:(j + 1) * T], ident[0:98, 0:98])
                    nc.tensor.transpose(t[0:T, 98:196], raw_ggs[m][:, S + j * T:S + (j + 1) * T], ident[0:98, 0:98])\
                        .then_inc(sem("prep_filled"), 1)
                    n += 1
            for m in range(MT):
                for j0, j1_ in QUART:
                    t = prep_bank()
                    for j in range(j0, j1_):
                        last = nc.tensor.transpose(t[0:T, (j - j0) * 128:(j - j0 + 1) * 128],
                                                   rawc_all[m][:, j * T:(j + 1) * T], ident[:, :])
                    last.then_inc(sem("prep_filled"), 1)
                    n += 1
            nc.tensor.transpose(gbank[0][0:C, 0:96], raw_w3[:, :], ident[0:96, 0:96])
            for i in range(2):
                nc.tensor.transpose(gbank[0][0:128, 128 + 64 * i:128 + 64 * i + DS], pad_ws1[:, 128 * i:128 * i + 128],
                                    ident[0:DS, 0:DS])
            for i in range(2):
                nc.tensor.transpose(gbank[0][0:C, 256 + 32 * i:288 + 32 * i], raw_ggc[:, i * C:(i + 1) * C],
                                    ident[0:IC, 0:IC])
            nc.tensor.transpose(gbank[0][0:IC, 320:320 + DC], raw_wc1[:, 1:1 + IC], ident[0:DC, 0:DC])
            for i in range(3):
                last = nc.tensor.transpose(gbank[0][0:128, 336 + 8 * i:336 + 8 * i + DC], pad_wc1[:, i, :],
                                           ident[0:DC, 0:DC])
            last.then_inc(sem("small_filled"), 1)
            pe.wait_ge(sem("weights_ready"), 1)
            pe.wait_ge(sem("wch_ready"), 2 * MT)
            pe.wait_ge(sem("wcl_ready"), 2 * MT)
            pe.wait_ge(sem("weh_ready"), 1)
            pe.wait_ge(sem("sel_ready"), 4)
            pe.wait_ge(sem("bias_stacked"), 16 * 9)
            pe.wait_ge(sem("cleared"), 4)

            def experts(pe, k, p, back, lo, hi):
                for n in range(lo, hi):
                    if live(k, p, back):
                        b, q = PIECES[n // E]
                        w = width(n)
                        src = gt[(p - back) % 2]
                        if n % 2:
                            m, mb = ago(n, 2, back)
                            need(pe, "prod_ready", k, p, m + 1, back=mb)
                            dst = gbank[2]
                        else:
                            m, mb = ago(n, 4, back)
                            need(pe, "lo_ready", k, p, m // 2 + 1, back=mb)
                            dst = gbank[(n // 2) % 2]
                        nc.tensor.matmul(dst[:, 0:w], selg[:, n % E, :], src[:, b, cols(q)],
                                         start=True, stop=True).then_inc(sem("gate_seen"), 1)
                    m, mb = ago(n, LAG, back)
                    if live(k, p, mb):
                        b, q = PIECES[m // E]
                        e = m % E
                        w = width(m)
                        dst = acc[(m // E) % 2]
                        if e == 0:
                            c, cb = (m // E - 1, mb) if m >= 2 * E else (m // E + 3, mb + 1)
                            need(pe, "out_ready", k, p, c, back=cb)
                            nc.tensor.matmul(dst[:, 0:w], bstk[:, :], gt[(p - mb) % 2][:, b, cols(q)],
                                             start=True, stop=False)
                        need(pe, "hi_ready", k, p, m + 1, back=mb)
                        nc.tensor.matmul(dst[:, 0:w], weh[:, e, :], prod_h[:, m % RING, 0:w], start=False, stop=False)
                        nc.tensor.matmul(dst[:, 0:w], wel[:, e, :], prod_h[:, m % RING, 0:w], start=False, stop=False)
                        need(pe, "lo_pool_ready" if m % 2 else "lo_ready", k, p, m // 2 + 1, back=mb)
                        nc.tensor.matmul(dst[:, 0:w], weh[:, e, :], prod_l[:, m % RING, 0:w], start=False,
                                         stop=(e == E - 1)).then_inc(sem("exp_done"), 1)

            def step(pe, k, p):
                core, front, route = live(k, p, 0), live(k, p, -1), live(k, p, 1)
                o = 1 - p

                def old(lo, hi):
                    experts(pe, k, p, 2, lo, hi)

                def new(lo, hi):
                    experts(pe, k, p, 1, lo, hi)

                def done(ins, use):
                    ins.then_inc(sem(USES[INDEX[use]][1] + "_filled"), 1)

                def to_tokens(kind, src, b, q):
                    for j in range(*QUART[q]):
                        last = nc.tensor.transpose(bank(f"{kind}{b}{q}", p)[0:T, (j - QUART[q][0]) * C:][:, 0:C],
                                                   src[:, b, j * T:(j + 1) * T], ident[:, :])
                    done(last, f"{kind}{b}{q}")

                def to_channels(kind, src, b, q):
                    for j in range(*QUART[q]):
                        last = nc.tensor.transpose(bank(f"{kind}{b}{q}", p)[:, (j - QUART[q][0]) * T:][:, 0:T],
                                                   src[:, j, b, :], ident[0:T, 0:T])
                    done(last, f"{kind}{b}{q}")

                def x2_tokens(b):
                    for q in range(2):
                        free(pe, f"x2_tok{b}{q}", k, p)
                        need(pe, "x2_ready", k, p, 2 * b + q + 1, back=1)
                        to_tokens("x2_tok", x2[o], b, q)

                if route:
                    x2_tokens(0)
                old(16, 17)
                if route:
                    x2_tokens(1)
                old(17, 18)
                if core:
                    for b, q in PIECES:
                        free(pe, f"tp{b}{q}", k, p)
                        need(pe, "y_ch_ready", k, p, 2 * b + q + 1)
                        w = (QUART[q][1] - QUART[q][0]) * T
                        done(nc.tensor.matmul(bank(f"tp{b}{q}", p)[0:96, 0:w], w3[:, :], y_ch[:, b, cols(q)],
                                              start=True, stop=True), f"tp{b}{q}")
                old(18, 20)
                if core:
                    for q in range(2):
                        free(pe, f"tp_tok{q}", k, p)
                        need(pe, "tp_ready", k, p, 3 + q)
                        for j in range(*QUART[q]):
                            last = nc.tensor.transpose(bank(f"tp_tok{q}", p)[0:T, (j - QUART[q][0]) * 128:][:, 0:128],
                                                       tp[:, j * T:(j + 1) * T], ident[:, :])
                        done(last, f"tp_tok{q}")
                old(20, 21)
                if route:
                    for b, q in PIECES:
                        free(pe, f"mean{b}{q}", k, p)
                        need(pe, "mean2_ready", k, p, 1, back=1)
                        for j in range(*QUART[q]):
                            i = NT * b + j
                            last = nc.tensor.transpose(bank(f"mean{b}{q}", p)[:, (j - QUART[q][0]) * T:][:, 0:T],
                                                       mean2[:, i:i + 1].to_broadcast([T, 128]), ident[0:T, 0:T])
                        done(last, f"mean{b}{q}")
                if core:
                    free(pe, "mix", k, p)
                    need(pe, "tp_tok_ready", k, p, 2)
                    for j in range(NT):
                        last = nc.tensor.matmul(bank("mix", p)[:, 0:2 * IS], tp_tok[:, j, :], wggs[:, j, :],
                                                start=(j == 0), stop=(j == NT - 1))
                    done(last, "mix")
                old(21, 23)
                if route:
                    free(pe, "rlogit", k, p)
                    for b in range(2):
                        need(pe, "centred_ready", k, p, 2 * b + 2, back=1)
                        for j in range(NT):
                            i = NT * b + j
                            last = nc.tensor.matmul(bank("rlogit", p)[0:T, E * i:E * i + E],
                                                    cen[o][:, b, j * T:(j + 1) * T], wr[:, :], start=True, stop=True)
                    done(last, "rlogit")

                def joint(q):
                    for b in range(2):
                        for m, (lo, hi) in enumerate(((0, 128), (128, IS))):
                            use = f"joint{b}{q}{m}"
                            free(pe, use, k, p)
                            rows = slice(64 * b, 64 * b + 64)
                            w = (QUART[q][1] - QUART[q][0]) * T
                            dst = bank(use, p)[0:hi - lo, 0:w]
                            need(pe, "mix_hi_ready", k, p, b + 1)
                            need(pe, "mix_lo_ready", k, p, b + 1)
                            need(pe, "tp_hi_ready", k, p, 2 * q + b + 1)
                            nc.tensor.matmul(dst, mix_s[b][:, lo:hi], tp_h[b][:, cols(q)], start=True, stop=False)
                            need(pe, "tp_lo_ready", k, p, 2 * q + b + 1)
                            done(nc.tensor.matmul(dst, mix_s[b][rows, lo:hi], tp_l[rows, cols(q)],
                                                  start=False, stop=True), use)

                def hidden(q):
                    use = f"hid{q}"
                    free(pe, use, k, p)
                    need(pe, "joint_ready", k, p, 4 * q + 4)
                    w = (QUART[q][1] - QUART[q][0]) * T
                    for b in range(2):
                        dst = bank(use, p)[64 * b:64 * b + 64, 0:w]
                        nc.tensor.matmul(dst, wws1[:, 0, :], j1[:, b, cols(q)], start=True, stop=False)
                        last = nc.tensor.matmul(dst, wws1[:, 1, :], j2[:, b, cols(q)], start=False, stop=True)
                    done(last, use)

                def x_tokens(b):
                    if b == 0:
                        pe.wait_ge(sem(f"x_loaded{o}"), (k + p) * 16 + 16)
                    for q in range(2):
                        free(pe, f"x_tok{b}{q}", k, p)
                        to_tokens("x_tok", x[o], b, q)

                if core:
                    joint(0)
                if front:
                    x_tokens(0)
                old(23, 24)
                if core:
                    joint(1)
                old(24, 25)
                if core:
                    hidden(0)
                old(25, 26)
                if core:
                    hidden(1)
                if front:
                    x_tokens(1)
                if core:
                    free(pe, "slogit", k, p)
                    need(pe, "hid_ready", k, p, 2)
                    for j in range(NT):
                        last = nc.tensor.matmul(bank("slogit", p)[0:T, j:j + NT + 1:NT], hid[:, j * T:(j + 1) * T],
                                                wws2[:, :], start=True, stop=True)
                    done(last, "slogit")
                old(26, 28)
                if route:
                    for b in range(2):
                        free(pe, f"gates{b}", k, p)
                        need(pe, "part", k, p, PART, back=1)
                        for j in range(NT):
                            last = nc.tensor.transpose(bank(f"gates{b}", p)[:, :].bitcast(BF16)[0:KR, j * T:(j + 1) * T],
                                                       gs[:, NT * b + j, :, :, :].rearrange("p i k e -> p (i k e)"),
                                                       identb[0:T, 0:T])
                        done(last, f"gates{b}")
                old(28, 32)
                if live(k, p, 1):
                    need(pe, "gates_ready", k, p, 2, back=1)
                new(0, 1)

                def channels(g):
                    free(pe, f"chan{g}", k, p)
                    for m in range(2 * g, min(2 * g + 2, MT)):
                        dst = bank(f"chan{g}", p)[:, 256 * (m % 2):256 * (m % 2) + 256]
                        rows = slice(m * 128, (m + 1) * 128)
                        for g2, (lo, hi) in enumerate(QUART):
                            if m == 0:
                                need(pe, "x1_hi_ready", k, p, g2 + 1)
                            for j in range(lo, hi):
                                xh = x1h[:, j, :, :].rearrange("p b c -> p (b c)")
                                nc.tensor.matmul(dst, wch[:, j, rows], xh, start=(j == 0), stop=False)
                                nc.tensor.matmul(dst, wcl[:, j, rows], xh, start=False, stop=False)
                        if m == 0:
                            new(1, 2)
                        for g2, (lo, hi) in enumerate(QUART):
                            if m == 0:
                                need(pe, "x1_lo_ready", k, p, g2 + 1)
                            for j in range(lo, hi):
                                last = nc.tensor.matmul(dst, wch[:, j, rows],
                                                        x1l[:, j, :, :].rearrange("p b c -> p (b c)"),
                                                        start=False, stop=(j == NT - 1))
                    done(last, f"chan{g}")

                if core:
                    channels(0)
                else:
                    new(1, 2)
                new(2, 3)
                if core:
                    channels(1)
                new(3, 5)
                if core:
                    channels(2)
                new(5, 6)
                if core:
                    free(pe, "gram", k, p)
                    need(pe, "chan_ready", k, p, 2)
                    for way in range(2):
                        for b in range(2):
                            dst = bank("gram", p)[:, 256 * way + 128 * b:256 * way + 128 * b + 128]
                            for i, rows in ((0, 128), (2, TAIL)):
                                last = nc.tensor.matmul(dst, chan[0:rows, i + way, b, :], chan[0:rows, i + 1 - way, b, :],
                                                        start=(i == 0), stop=(i == 2))
                    done(last, "gram")
                if front:
                    for q in range(2):
                        free(pe, f"y_ch0{q}", k, p)
                        need(pe, "y_tok_ready", k, p, q + 1, back=-1)
                        to_channels("y_ch", tok[o], 0, q)
                new(6, 8)
                if core:
                    free(pe, "jc", k, p)
                    need(pe, "gram_ready", k, p, 1)
                    for way in range(2):
                        last = nc.tensor.matmul(bank("jc", p)[0:IC, 0:256], wggc[:, way, :],
                                                gram[:, 1 - way, :, :].rearrange("p b c -> p (b c)"),
                                                start=(way == 0), stop=(way == 1))
                    done(last, "jc")
                if front:
                    free(pe, "y_ch10", k, p)
                    need(pe, "y_tok_ready", k, p, 3, back=-1)
                    to_channels("y_ch", tok[o], 1, 0)
                new(8, 9)
                if core:
                    free(pe, "hc", k, p)
                    need(pe, "jc_ready", k, p, 1)
                    need(pe, "chan_ready", k, p, 3)
                    dst = bank("hc", p)[0:DC, 0:256]
                    for i, rows in ((2, 128), (3, 128), (4, GX5)):
                        nc.tensor.matmul(dst, wwc1g[0:rows, i - 2, :], chan[0:rows, i, :, :].rearrange("p b c -> p (b c)"),
                                         start=(i == 2), stop=False)
                    done(nc.tensor.matmul(dst, wwc1[:, :], jc[:, :, :].rearrange("p b c -> p (b c)"),
                                          start=False, stop=True), "hc")
                if front:
                    free(pe, "y_ch11", k, p)
                    need(pe, "y_tok_ready", k, p, 4, back=-1)
                    to_channels("y_ch", tok[o], 1, 1)
                new(9, 10)
                if core:
                    free(pe, "clogit", k, p)
                    need(pe, "hc_ready", k, p, 1)
                    for b in range(2):
                        last = nc.tensor.matmul(bank("clogit", p)[:, b:b + 1], hc[:, b, :], wwc2[:, :],
                                                start=True, stop=True)
                    done(last, "clogit")
                new(10, 12)
                if core:
                    for b, q in PIECES:
                        free(pe, f"x1_ch{b}{q}", k, p)
                        to_channels("x1_ch", tok[p], b, q)
                        new(12 + 2 * b + q, 13 + 2 * b + q)
                else:
                    new(12, 16)

            steps(pe, step)

        @block.vector
        def _(dve):
            dve.wait_ge(sem("weights_loaded"), 16 * len(small))
            for m in range(2):
                nc.vector.tensor_scalar(raw_ggs[m], raw_ggs[m], raw_sggs[:, m:m + 1], None, ALU.mult)
            for m in range(MT):
                nc.vector.tensor_scalar(rawc_all[m], rawc_all[m], raw_sc[:, m:m + 1], None, ALU.mult)
            nc.vector.tensor_scalar(raw_w3[:, :], raw_w3[:, :], raw_s3[:, :], None, ALU.mult)
            nc.vector.memset(pad_ws1[:, :], 0.0)
            nc.vector.memset(pad_wc1[:, :, :], 0.0)
            nc.vector.tensor_scalar(raw_ws1[:, :], raw_ws1[:, :], raw_sws1[:, :], None, ALU.mult)
            nc.vector.tensor_scalar(raw_ggc[:, :], raw_ggc[:, :], raw_sggc[:, :], None, ALU.mult)
            nc.vector.tensor_scalar(raw_wc1[:, :], raw_wc1[:, :], raw_swc1[:, :], None, ALU.mult)\
                .then_inc(sem("prep_step"), 1)
            dve.wait_ge(sem("prep_step"), 1)
            nc.vector.tensor_copy(pad_ws1[:, 0:IS], raw_ws1[:, 1:1 + IS])
            nc.vector.tensor_scalar(pad_ws1[:, 224:256], raw_ws1[:, 0:1].to_broadcast([DS, IC]), 1.0 / IC, None,
                                    ALU.mult)
            for i, (lo, hi) in enumerate(((TAIL, 128), (TAIL, 128), (0, GX5))):
                last = nc.vector.tensor_scalar(pad_wc1[:, i, lo:hi], raw_wc1[:, 0:1].to_broadcast([DC, hi - lo]),
                                               1.0 / IS, None, ALU.mult)
            last.then_inc(sem("rows_scaled"), 1)
            nc.vector.tensor_scalar(sbs[:, :], raw_sbs[:, :], -1.0, None, ALU.mult)
            nc.vector.tensor_scalar(sbc[:, :], raw_sbc[:, :], -1.0, None, ALU.mult)
            for e in range(E):
                nc.vector.memset(pref[:, e:e + 1], float(E - e))
            nc.vector.tensor_copy(eb[:, 0, :], raw_eb[:, :]).then_inc(sem("bias_parts_ready"), 1)
            dve.wait_ge(sem("bias_parts_ready"), 1)
            nc.vector.tensor_tensor(res_eb[:, :], raw_eb[:, :], eb[:, 0, :], ALU.subtract).then_inc(sem("prep_step"), 1)
            dve.wait_ge(sem("prep_step"), 2)
            nc.vector.tensor_copy(eb[:, 1, :], res_eb[:, :]).then_inc(sem("bias_parts_ready"), 1)
            dve.wait_ge(sem("bias_parts_ready"), 2)
            nc.vector.tensor_tensor(raw_eb[:, :], res_eb[:, :], eb[:, 1, :], ALU.subtract).then_inc(sem("prep_step"), 1)
            dve.wait_ge(sem("prep_step"), 3)
            nc.vector.tensor_copy(eb[:, 2, :], raw_eb[:, :]).then_inc(sem("bias_parts_ready"), 1)
            n = 0
            for m in range(MT):
                for j0, j1_ in QUART:
                    dve.wait_ge(sem("wch_ready"), n + 1)
                    dst = slice(m * 128, (m + 1) * 128)
                    src = rot[(2 * NT + n) % NB][0:T, 0:(j1_ - j0) * 128].rearrange("p (j c) -> p j c", c=128)
                    nc.vector.tensor_tensor(wcl[:, j0:j1_, dst], src, wch[:, j0:j1_, dst].bitcast(F32), ALU.subtract)\
                        .then_inc(sem("wcl_ready"), 1)
                    n += 1
            dve.wait_ge(sem("small_filled"), 1)
            g = gbank[0]
            nc.vector.tensor_copy(w3[:, :], g[:, 0:96])
            nc.vector.memset(wws1[:, :, :], 0.0).then_inc(sem("prep_step"), 1)
            dve.wait_ge(sem("prep_step"), 4)
            nc.vector.tensor_copy(wws1[:, :, 0:DS], g[:, 128:256].rearrange("p (i c) -> p i c", i=2)[:, :, 0:DS])
            nc.vector.tensor_copy(wggc[:, :, :], g[:, 256:320].rearrange("p (i c) -> p i c", i=2))
            nc.vector.tensor_copy(wwc1[:, :], g[0:IC, 320:320 + DC])
            nc.vector.tensor_copy(wwc1g[:, :, :], g[:, 336:360].rearrange("p (i c) -> p i c", i=3))
            dve.wait_ge(sem("weh_ready"), 1)
            nc.vector.tensor_tensor(wel[:, :, :], raw_we, weh[:, :, :].bitcast(F32), ALU.subtract)\
                .then_inc(sem("weights_ready"), 1)
            dve.wait_ge(sem("weights_ready"), 1)

            def experts(dve, k, p, back, lo, hi):
                for n in range(lo, hi):
                    if n % E == LAG + 1:
                        m, mb = ago(n, LAG + 1 + E, back)
                        if live(k, p, mb):
                            c = m // E
                            b, q = PIECES[c]
                            w = width(m)
                            dst = x2[(p - mb) % 2][:, b, cols(q)]
                            need(dve, "exp_done", k, p, E * (c + 1), back=mb)
                            nc.vector.tensor_tensor(dst, acc[c % 2][:, 0:w], dst, ALU.add).then_inc(sem("out_ready"), 1)
                    if live(k, p, back):
                        b, q = PIECES[n // E]
                        w = width(n)
                        src = cen[(p - back) % 2][:, b, cols(q)]
                        if n % 2:
                            m, mb = ago(n, 4, back)
                            need(dve, "lo_pool_ready", k, p, m // 2 + 1, back=mb)
                            need(dve, "gate_seen", k, p, n + 1, back=back)
                            nc.vector.tensor_tensor(prod[:, (n // 2) % 4, 0:w], gbank[2][:, 0:w], src, ALU.mult)\
                                .then_inc(sem("prod_ready"), 1)
                        else:
                            g = gbank[(n // 2) % 2][:, 0:w]
                            need(dve, "gate_seen", k, p, n + 1, back=back)
                            nc.vector.tensor_tensor(g, g, src, ALU.mult).then_inc(sem("prod_ready"), 1)
                    m, mb = ago(n, 1, back)
                    if m % 2 == 0 and live(k, p, mb):
                        w = width(m)
                        need(dve, "hi_ready", k, p, m + 1, back=mb)
                        nc.vector.tensor_tensor(prod_l[:, m % RING, 0:w], gbank[(m // 2) % 2][:, 0:w],
                                                prod_h[:, m % RING, 0:w].bitcast(F32), ALU.subtract)\
                            .then_inc(sem("lo_ready"), 1)

            def step(dve, k, p):
                core, front, route = live(k, p, 0), live(k, p, -1), live(k, p, 1)
                o = 1 - p
                count = [0]

                def old(lo, hi):
                    experts(dve, k, p, 2, lo, hi)

                def new(lo, hi):
                    experts(dve, k, p, 1, lo, hi)

                def then(ins, name, back):
                    count[0] += 1
                    ins.then_inc(sem(name), 1)
                    need(dve, name, k, p, count[0], back=back)

                def moments(sm, mean, var, eps, name, ready, back):
                    me, mo, ve, vo = st[:, :, 1], st[:, :, 4], st[:, :, 2], st[:, :, 5]
                    nc.vector.tensor_tensor(sm[:, 0, :], me, mo, ALU.subtract).then_inc(sem(name), 1)
                    nc.vector.tensor_tensor(sm[:, 1, :], ve, vo, ALU.add).then_inc(sem(name), 1)
                    nc.vector.tensor_tensor(sm[:, 2, :], me, mo, ALU.add).then_inc(sem(name), 1)
                    count[0] += 3
                    need(dve, name, k, p, count[0], back=back)
                    then(nc.vector.tensor_tensor(sm[:, 3, :], sm[:, 0, :], sm[:, 0, :], ALU.mult), name, back)
                    then(nc.vector.scalar_tensor_tensor(out=sm[:, 4, :], in0=sm[:, 3, :], scalar=C / 4.0,
                                                        in1=sm[:, 1, :], op0=ALU.mult, op1=ALU.add), name, back)
                    then(nc.vector.tensor_scalar(mean[:, :], sm[:, 2, :], 0.5, None, ALU.mult), name, back)
                    nc.vector.tensor_scalar(var[:, :], sm[:, 4, :], 1.0 / C, eps, ALU.mult, ALU.add)\
                        .then_inc(sem(ready), 1)
                    need(dve, ready, k, p, 1, back=back)

                def stats2(b):
                    for q in range(2):
                        filled(dve, f"x2_tok{b}{q}", k, p)
                        for j in range(*QUART[q]):
                            last = nc.vector.bn_stats(st[:, NT * b + j, :],
                                                      bank(f"x2_tok{b}{q}", p)[0:T, (j - QUART[q][0]) * C:][:, 0:C])
                        last.then_inc(sem("stats2_ready"), 1)

                def stats1(b):
                    need(dve, "xt_ready", k, p, 2 * b + 2, back=-1)
                    for j in range(NT):
                        last = nc.vector.bn_stats(st[:, NT * b + j, :], tok[o][:, j, b, :])
                    last.then_inc(sem("stats1_read"), 1)

                def normalise(b):
                    for lo, hi in QUART:
                        for j in range(lo, hi):
                            i = NT * b + j
                            last = nc.vector.tensor_scalar(tok[o][:, j, b, :], tok[o][:, j, b, :], mean1[:, i:i + 1],
                                                           rstd1[:, i:i + 1], ALU.subtract, ALU.mult)
                        last.then_inc(sem("y_tok_ready"), 1)

                def centre(b):
                    for q in range(2):
                        filled(dve, f"mean{b}{q}", k, p)
                        w = (QUART[q][1] - QUART[q][0]) * T
                        nc.vector.tensor_tensor(cen[o][:, b, cols(q)], x2[o][:, b, cols(q)],
                                                bank(f"mean{b}{q}", p)[:, 0:w], ALU.subtract)\
                            .then_inc(sem("centred_ready"), 1)

                if route:
                    stats2(0)
                old(16, 17)
                if route:
                    stats2(1)
                old(17, 18)
                if route:
                    need(dve, "stats2_ready", k, p, 4, back=1)
                    moments(sm, mean2, var2, EPS2, "stat2", "mean2_ready", 1)
                    assert count[0] == STAT
                old(18, 21)
                if route:
                    centre(0)
                    centre(1)
                old(21, 22)
                if core:
                    for b in range(2):
                        need(dve, "mix_hi_ready", k, p, b + 1)
                        rows = slice(64 * b, 64 * b + 64)
                        nc.vector.tensor_tensor(mix_s[b][64 - 64 * b:128 - 64 * b, :], mix[rows, :],
                                                mix_s[b][rows, :].bitcast(F32), ALU.subtract)\
                            .then_inc(sem("mix_lo_ready"), 1)
                old(22, 23)

                def tiles(v):
                    return v.unsqueeze(2).to_broadcast([T, 2 * NT, E])

                def each(v):
                    return v.unsqueeze(1).to_broadcast([T, 2 * NT, E])

                def link(ins):
                    then(ins, "route", 1)

                def pick(logits, top, hot):
                    link(nc.vector.tensor_tensor(eq[:, :, :], logits[:, :, :], tiles(top), ALU.is_equal))
                    link(nc.vector.tensor_tensor(eq[:, :, :], eq[:, :, :], each(pref[:, :]), ALU.mult))
                    link(nc.vector.tensor_reduce(mx[:, 4, :], eq[:, :, :], AX_X, ALU.max))
                    link(nc.vector.tensor_tensor(hot[:, :, :], eq[:, :, :], tiles(mx[:, 4, :]), ALU.is_equal))

                def flat(v):
                    return v[:, :, :].rearrange("p i e -> p (i e)")

                if route:
                    count[0] = 0
                    need(dve, "rstd2_ready", k, p, 1, back=1)
                    filled(dve, "rlogit", k, p)
                    src = bank("rlogit", p)[0:T, 0:2 * NT * E].rearrange("p (i e) -> p i e", e=E)
                    nc.vector.tensor_tensor(lg[:, :, :], src, tiles(rstd2[:, :]), ALU.mult)\
                        .then_inc(sem("rlogit_read"), 1)
                    need(dve, "rlogit_read", k, p, 1, back=1)
                    link(nc.vector.tensor_tensor(lg[:, :, :], lg[:, :, :], each(rb[:, :]), ALU.add))
                    link(nc.vector.tensor_reduce(mx[:, 0, :], lg[:, :, :], AX_X, ALU.max))
                    pick(lg, mx[:, 0, :], first)
                    link(nc.vector.scalar_tensor_tensor(out=flat(lg2), in0=flat(first), scalar=-BIG, in1=flat(lg),
                                                        op0=ALU.mult, op1=ALU.add))
                    link(nc.vector.tensor_reduce(mx[:, 1, :], lg2[:, :, :], AX_X, ALU.max))
                    nc.vector.tensor_tensor(mx[:, 2, :], mx[:, 1, :], mx[:, 0, :], ALU.subtract)\
                        .then_inc(sem("rgap_ready"), 1)
                    pick(lg2, mx[:, 1, :], second)
                old(23, 24)
                if route:
                    need(dve, "rexp_ready", k, p, 1, back=1)
                    link(nc.vector.tensor_scalar(mx[:, 5, :], mx[:, 3, :], 1.0, None, ALU.add))
                    link(nc.vector.reciprocal(mx[:, 6, :], mx[:, 5, :]))
                    link(nc.vector.tensor_tensor(mx[:, 7, :], mx[:, 6, :], mx[:, 3, :], ALU.mult))
                    link(nc.vector.tensor_tensor(first[:, :, :], first[:, :, :], tiles(mx[:, 6, :]), ALU.mult))
                    link(nc.vector.tensor_tensor(second[:, :, :], second[:, :, :], tiles(mx[:, 7, :]), ALU.mult))
                    link(nc.vector.tensor_tensor(gv[:, :, 1, :], first[:, :, :], second[:, :, :], ALU.add))
                    nc.vector.tensor_tensor(gv[:, :, 0, :], gv[:, :, 1, :], tiles(rstd2[:, :]), ALU.mult)\
                        .then_inc(sem("gatev_ready"), 1)
                    assert count[0] == ROUTE, count[0]
                old(24, 26)
                if front:
                    stats1(0)
                if core:
                    filled(dve, "slogit", k, p)
                    nc.vector.tensor_scalar(sp1[:, :], bank("slogit", p)[0:T, 0:2 * NT], sbs[:, 0:1], sbs[:, 1:2],
                                            ALU.mult, ALU.add).then_inc(sem("slogit_read"), 1)
                    need(dve, "slogit_read", k, p, 1)
                    nc.vector.tensor_scalar(sz[:, :], sp1[:, :], 85.0, None, ALU.min).then_inc(sem("szlogit_ready"), 1)
                old(26, 27)
                if core:
                    need(dve, "sexp_ready", k, p, 1)
                    nc.vector.tensor_scalar(sp1[:, :], se[:, :], 1.0, None, ALU.add).then_inc(sem("sgate"), 1)
                    need(dve, "sgate", k, p, 1)
                    nc.vector.reciprocal(sig[:, :], sp1[:, :]).then_inc(sem("sgate"), 1)
                    need(dve, "sgate", k, p, 2)
                    for g, (lo, hi) in enumerate(QUART):
                        for j in range(lo, hi):
                            for b in range(2):
                                i = NT * b + j
                                last = nc.vector.tensor_scalar(tok[p][:, j, b, :], tok[p][:, j, b, :], sig[:, i:i + 1],
                                                               None, ALU.mult)
                        last.then_inc(sem("x1_ready"), 1)
                        old(27 + 2 * g, 29 + 2 * g)
                else:
                    old(27, 31)
                old(31, 32)
                if front:
                    stats1(1)
                    need(dve, "stats1_read", k, p, 2, back=-1)
                    count[0] = 0
                    moments(sm, mean1, var1, EPS1, "stat1", "stats1_ready", -1)
                    assert count[0] == STAT
                new(0, 3)
                if front:
                    need(dve, "rstd1_ready", k, p, 1, back=-1)
                    normalise(0)
                new(3, 4)
                if front:
                    normalise(1)
                new(4, 10)
                if core:
                    filled(dve, "clogit", k, p)
                    nc.vector.tensor_scalar(cz[:, 0, :], bank("clogit", p)[:, 0:2], sbc[:, 0:1], sbc[:, 1:2],
                                            ALU.mult, ALU.add).then_inc(sem("clogit_read"), 1)
                    need(dve, "clogit_read", k, p, 1)
                    nc.vector.tensor_scalar(cz[:, 1, :], cz[:, 0, :], 85.0, None, ALU.min)\
                        .then_inc(sem("czlogit_ready"), 1)
                new(10, 12)
                if core:
                    need(dve, "cexp_ready", k, p, 1)
                    nc.vector.tensor_scalar(cz[:, 3, :], cz[:, 2, :], 1.0, None, ALU.add).then_inc(sem("cgate"), 1)
                    need(dve, "cgate", k, p, 1)
                    nc.vector.reciprocal(cg[:, :], cz[:, 3, :]).then_inc(sem("cgate"), 1)
                    need(dve, "cgate", k, p, 2)
                    if not isinstance(k, int) or k > 0:
                        dve.wait_ge(sem(f"stored{p}"), k * (16 * PAIR))
                    for b, q in PIECES:
                        filled(dve, f"x1_ch{b}{q}", k, p)
                        w = (QUART[q][1] - QUART[q][0]) * T
                        nc.vector.scalar_tensor_tensor(out=x2[p][:, b, cols(q)], in0=bank(f"x1_ch{b}{q}", p)[:, 0:w],
                                                       scalar=cg[:, b:b + 1], in1=x[p][:, b, cols(q)],
                                                       op0=ALU.mult, op1=ALU.add).then_inc(sem("x2_ready"), 1)
                        new(12 + 2 * b + q, 13 + 2 * b + q)
                else:
                    new(12, 16)

            steps(dve, step)


_CONV = [f"{n}_{k}" for n in ("th", "ph", "ggs", "gxs", "ws1", "ws2", "thc", "phc", "ggc", "gxc", "wc1", "wc2")
         for k in ("w", "s", "b")]
_INS = {"x": "x"}
_INS.update({n: "L0_conv_" + n for n in _CONV})
_INS.update({n: "L0_ffn_" + n for n in ("router_w", "router_b", "expert_w", "expert_b")})


def kernel(**inputs):
    import numpy as _np
    import concourse.bacc as _bacc
    from concourse import mybir as _mybir
    from concourse.bass_utils import run_bass_kernel_spmd as _run

    nc = _bacc.Bacc("TRN2", target_bir_lowering=False, num_devices=1)
    arrays, args = {}, {}
    for short, name in _INS.items():
        v = _np.ascontiguousarray(inputs[name])
        arrays[f"in_{short}"] = v
        args[short] = nc.dram_tensor(f"in_{short}", v.shape, _mybir.dt.from_np(v.dtype), kind="ExternalInput").ap()
    o = nc.dram_tensor("out_0", (BATCH, C, HH, WW), _mybir.dt.float32, kind="ExternalOutput").ap()
    metaformer_kernel(nc, args, o)
    r = _run(nc, [arrays], core_ids=[0])
    return r.results[0]["out_0"]
```
